# Optimizing a Trainium2 kernel written in Bass

```python
import numpy as np
import jax
import jax.numpy as jnp

def _softmax(x, axis=-1):
    return jax.nn.softmax(x, axis=axis)

def _gelu(x):
    return jax.nn.gelu(x, approximate=True)

def _silu(x):
    return jax.nn.silu(x)

def _sigmoid(x):
    return jax.nn.sigmoid(x)

def _layernorm(x, axis=-1, eps=1e-05):
    m = jnp.mean(x, axis=axis, keepdims=True)
    v = jnp.var(x, axis=axis, keepdims=True)
    return (x - m) / jnp.sqrt(v + eps)

def _scatter_add(tgt, idx, src, axis=0):
    return tgt.at[idx].add(src)

def _segment_sum(src, seg, n):
    return jax.ops.segment_sum(src, seg, n)
kernel_name = 'mk_prb_d1_jaxref_r4_11a083'

def setup_inputs(seed: int=0):
    np.random.seed(seed)
    _w = jnp.asarray

    def _L0_attn_setup():
        import jax, jax.numpy as jnp
        import numpy as np
        import math
        D = 256
        CHUNK = 64
        B = 4
        S = 1024

        def _layernorm(x, g, b, eps=1e-05):
            mu = jnp.mean(x, axis=-1, keepdims=True)
            var = jnp.mean((x - mu) ** 2, axis=-1, keepdims=True)
            return (x - mu) * jax.lax.rsqrt(var + eps) * g + b
        key = jax.random.key(seed)
        ks = jax.random.split(key, 8)
        lin = lambda k: jax.random.normal(k, (D, D), jnp.float32) * 0.02
        return {'x': jax.random.normal(ks[0], (B, S, D), jnp.float32), 'Wk': lin(ks[1]), 'bk': jnp.zeros((D,), jnp.float32), 'Wv': lin(ks[2]), 'bv': jnp.zeros((D,), jnp.float32), 'Wq': lin(ks[3]), 'bq': jnp.zeros((D,), jnp.float32), 'Wkp': lin(ks[4]), 'bkp': jnp.zeros((D,), jnp.float32), 'Wqp': lin(ks[5]), 'bqp': jnp.zeros((D,), jnp.float32), 'phase_scale': jnp.ones((D,), jnp.float32) * math.pi, 'ln_g': jnp.ones((D,), jnp.float32), 'ln_b': jnp.zeros((D,), jnp.float32), 'Wo': lin(ks[6]), 'bo': jnp.zeros((D,), jnp.float32)}
    _L0_attn_in = _L0_attn_setup()

    def _L0_ffn_setup():
        import math
        import jax, jax.numpy as jnp
        import numpy as np
        E = 8
        H = 256
        HP = 128
        SPARSITY = 8
        N_ROTATE = 64
        ROPE_BASE = 10000.0

        def _rope(x, pos):
            half = N_ROTATE // 2
            inv_freq = 1.0 / ROPE_BASE ** (jnp.arange(half, dtype=jnp.float32) * 2.0 / N_ROTATE)
            ang = pos.astype(jnp.float32)[..., None] * inv_freq
            sin, cos = (jnp.sin(ang), jnp.cos(ang))
            x1, x2 = (x[..., :half], x[..., half:])
            return jnp.concatenate([x1 * cos - x2 * sin, x2 * cos + x1 * sin], axis=-1)
        key = jax.random.key(seed)
        k1, k2, k3, k4 = jax.random.split(key, 4)
        B, T = (4, 2048)
        X = jax.random.normal(k1, (B, T, H), dtype=jnp.float32)
        Wr = jax.random.uniform(k2, (E, H), minval=-1 / math.sqrt(H), maxval=1 / math.sqrt(H), dtype=jnp.float32)
        bq = 1 / math.sqrt(3 * HP)
        Wqkv = jax.random.uniform(k3, (E, H, 3 * HP), minval=-bq, maxval=bq, dtype=jnp.float32)
        bo = 1 / math.sqrt(H * E)
        Wo = jax.random.uniform(k4, (E, HP, H), minval=-bo, maxval=bo, dtype=jnp.float32)
        return {'X': X, 'Wr': Wr, 'Wqkv': Wqkv, 'Wo': Wo}
    _L0_ffn_in = _L0_ffn_setup()
    _d = {'L0_attn_x': _L0_attn_in['x'], 'L0_attn_Wk': _L0_attn_in['Wk'], 'L0_attn_bk': _L0_attn_in['bk'], 'L0_attn_Wv': _L0_attn_in['Wv'], 'L0_attn_bv': _L0_attn_in['bv'], 'L0_attn_Wq': _L0_attn_in['Wq'], 'L0_attn_bq': _L0_attn_in['bq'], 'L0_attn_Wkp': _L0_attn_in['Wkp'], 'L0_attn_bkp': _L0_attn_in['bkp'], 'L0_attn_Wqp': _L0_attn_in['Wqp'], 'L0_attn_bqp': _L0_attn_in['bqp'], 'L0_attn_phase_scale': _L0_attn_in['phase_scale'], 'L0_attn_ln_g': _L0_attn_in['ln_g'], 'L0_attn_ln_b': _L0_attn_in['ln_b'], 'L0_attn_Wo': _L0_attn_in['Wo'], 'L0_attn_bo': _L0_attn_in['bo'], 'L0_ffn_Wr': _L0_ffn_in['Wr'], 'L0_ffn_Wqkv': _L0_ffn_in['Wqkv'], 'L0_ffn_Wo': _L0_ffn_in['Wo']}
    _x0 = _d['L0_attn_x']
    _d['L0_attn_x'] = jax.random.normal(jax.random.fold_in(jax.random.key(seed), 1), (16, 1024, 256), dtype=_x0.dtype)
    del _x0
    return _d

def reference(L0_attn_x, L0_attn_Wk, L0_attn_bk, L0_attn_Wv, L0_attn_bv, L0_attn_Wq, L0_attn_bq, L0_attn_Wkp, L0_attn_bkp, L0_attn_Wqp, L0_attn_bqp, L0_attn_phase_scale, L0_attn_ln_g, L0_attn_ln_b, L0_attn_Wo, L0_attn_bo, L0_ffn_Wr, L0_ffn_Wqkv, L0_ffn_Wo):

    def _L0_attn_ref(x, Wk, bk, Wv, bv, Wq, bq, Wkp, bkp, Wqp, bqp, phase_scale, ln_g, ln_b, Wo, bo):
        import jax, jax.numpy as jnp
        import numpy as np
        import math
        D = 256
        CHUNK = 64
        B = 4
        S = 1024

        def _layernorm(x, g, b, eps=1e-05):
            mu = jnp.mean(x, axis=-1, keepdims=True)
            var = jnp.mean((x - mu) ** 2, axis=-1, keepdims=True)
            return (x - mu) * jax.lax.rsqrt(var + eps) * g + b
        batch, seq_len, dim = x.shape
        key = jnp.einsum('bsd,ed->bse', x, Wk) + bk
        value = jnp.einsum('bsd,ed->bse', x, Wv) + bv
        query = jnp.einsum('bsd,ed->bse', x, Wq) + bq
        key_phase = jnp.tanh(jnp.einsum('bsd,ed->bse', key, Wkp) + bkp) * phase_scale
        query_phase = jnp.tanh(jnp.einsum('bsd,ed->bse', query, Wqp) + bqp) * phase_scale
        bound_real = value * jnp.cos(key_phase)
        bound_imag = value * jnp.sin(key_phase)
        pad_len = -seq_len % CHUNK
        if pad_len > 0:
            pad = ((0, 0), (0, pad_len), (0, 0))
            bound_real = jnp.pad(bound_real, pad)
            bound_imag = jnp.pad(bound_imag, pad)
            query_phase = jnp.pad(query_phase, pad)
        padded_len = seq_len + pad_len
        nc = padded_len // CHUNK
        br = bound_real.reshape(batch, nc, CHUNK, dim)
        bi = bound_imag.reshape(batch, nc, CHUNK, dim)
        qp = query_phase.reshape(batch, nc, CHUNK, dim)
        mem_real = jnp.cumsum(br, axis=2)
        mem_imag = jnp.cumsum(bi, axis=2)
        retrieved = mem_real * jnp.cos(qp) + mem_imag * jnp.sin(qp)
        retrieved = retrieved.reshape(batch, padded_len, dim)[:, :seq_len]
        retrieved = retrieved / math.sqrt(dim)
        out = jnp.einsum('bsd,ed->bse', _layernorm(retrieved, ln_g, ln_b), Wo) + bo
        return x + out

    def _L0_ffn_ref(X, Wr, Wqkv, Wo):
        import math
        import jax, jax.numpy as jnp
        import numpy as np
        E = 8
        H = 256
        HP = 128
        SPARSITY = 8
        N_ROTATE = 64
        ROPE_BASE = 10000.0

        def _rope(x, pos):
            half = N_ROTATE // 2
            inv_freq = 1.0 / ROPE_BASE ** (jnp.arange(half, dtype=jnp.float32) * 2.0 / N_ROTATE)
            ang = pos.astype(jnp.float32)[..., None] * inv_freq
            sin, cos = (jnp.sin(ang), jnp.cos(ang))
            x1, x2 = (x[..., :half], x[..., half:])
            return jnp.concatenate([x1 * cos - x2 * sin, x2 * cos + x1 * sin], axis=-1)
        B, T, _ = X.shape
        k = min(max(T // SPARSITY, 2), T)
        logits = jax.nn.sigmoid(jnp.einsum('bth,eh->bte', X, Wr))
        topk_vals, topk_I = jax.lax.top_k(logits.transpose(0, 2, 1), k)
        idx_flat = topk_I.reshape(B, E * k)
        Xg = jnp.take_along_axis(X, idx_flat[:, :, None], axis=1).reshape(B, E, k, H)
        QKV = jnp.einsum('beki,eij->bekj', Xg, Wqkv)
        Q, K, V = jnp.split(QKV, 3, axis=-1)
        Q = jnp.concatenate([_rope(Q[..., :N_ROTATE], topk_I), Q[..., N_ROTATE:]], axis=-1)
        K = jnp.concatenate([_rope(K[..., :N_ROTATE], topk_I), K[..., N_ROTATE:]], axis=-1)
        M = topk_I[..., :, None] >= topk_I[..., None, :]
        scores = jnp.einsum('bekd,bemd->bekm', Q, K) / math.sqrt(HP)
        scores = jnp.where(M, scores, -jnp.inf)
        A = jax.nn.softmax(scores, axis=-1)
        AV = jnp.einsum('bekm,bemd->bekd', A, V)
        AV = AV * topk_vals[..., None]
        Xpre = jnp.einsum('bekj,eji->beki', AV, Wo)
        out = jnp.zeros((B, T, H), dtype=X.dtype)
        out = out.at[jnp.arange(B)[:, None], idx_flat].add(Xpre.reshape(B, E * k, H))
        return out
    x = L0_attn_x
    xn = _layernorm(x, axis=-1)
    x = x + _L0_attn_ref(xn, L0_attn_Wk, L0_attn_bk, L0_attn_Wv, L0_attn_bv, L0_attn_Wq, L0_attn_bq, L0_attn_Wkp, L0_attn_bkp, L0_attn_Wqp, L0_attn_bqp, L0_attn_phase_scale, L0_attn_ln_g, L0_attn_ln_b, L0_attn_Wo, L0_attn_bo) + _L0_ffn_ref(xn, L0_ffn_Wr, L0_ffn_Wqkv, L0_ffn_Wo)
    return x

_drawn_inputs = setup_inputs


def setup_inputs(seed=0):
    import zlib

    import numpy as np

    out = dict(_drawn_inputs(seed))
    spreads = {'L0_attn_bk': (0.0, 0.8),
     'L0_attn_bv': (0.0, 0.1),
     'L0_attn_bq': (0.0, 0.8),
     'L0_attn_bkp': (0.0, 0.293),
     'L0_attn_bqp': (0.0, 0.1),
     'L0_attn_phase_scale': (3.1415927410125732, 0.6),
     'L0_attn_ln_g': (1.0, 0.6),
     'L0_attn_ln_b': (0.0, 0.483),
     'L0_attn_bo': (0.0, 0.372)}
    factors = {'L0_ffn_Wr': 8.0, 'L0_ffn_Wqkv': 8.0, 'L0_ffn_Wo': 8.0, 'L0_attn_Wk': 3.387}
    for name, (base, spread) in spreads.items():
        noise = np.random.default_rng([zlib.crc32(name.encode()), seed]).standard_normal(out[name].shape)
        drawn = base * np.exp(spread * noise) if base else spread * noise
        out[name] = jnp.asarray(drawn.astype(out[name].dtype))
    for name, factor in factors.items():
        out[name] = (out[name] * factor).astype(out[name].dtype)
    return out
```

```python
from contextlib import ExitStack

import numpy as np

import concourse.bass as bass
import concourse.mybir as mybir

F32 = mybir.dt.float32
BF16 = mybir.dt.bfloat16
I32 = mybir.dt.int32
I16 = mybir.dt.int16
U32 = mybir.dt.uint32
ALU = mybir.AluOpType
ACT = mybir.ActivationFunctionType
AX = mybir.AxisListType

P = 128
NB, SEQ, D = 16, 1024, 256
NTOK = NB * SEQ
CH = 64
FC = D // P
HALF = 512
TPH = HALF // P
TPB = SEQ // P
UNITS = NB * (SEQ // HALF) * FC
PAIRS = UNITS - 4
HALVES = UNITS // 2
E, HP, ROT = 8, 128, 64
RH = ROT // 2
K = SEQ // 8
GROW = D + 3 * RH
QW = 3 * HP + 1
EPS = 1e-5
TWO_PI = float(2 * np.pi)
ROUND = float(1.5 * 2 ** 23)
MASKED = -1e30
SCALE = float(HP) ** -0.5
EXPERT_UNITS = NB * E


def build(nc, x, Wk, bk, Wv, bv, Wq, bq, Wkp, bkp, Wqp, bqp, phase_scale, ln_g, ln_b, Wo, bo, Wr, Wqkv, Wfo,
          rope, out):
    with ExitStack() as ctx:
        def sb(name, shape, dt=F32):
            return ctx.enter_context(nc.sbuf_tensor(name, shape, dt))

        def sem(name):
            return ctx.enter_context(nc.semaphore(name))

        xn_rows = nc.dram_tensor("xn_rows", [NTOK, GROW], F32, kind="Internal").ap()
        logit_rows = nc.dram_tensor("logit_rows", [NB, E, SEQ], F32, kind="Internal").ap()

        ident = sb("ident", [P, P])
        ident_bf = sb("ident_bf", [P, P], BF16)
        causal = sb("causal", [P, K], BF16)
        ones = sb("ones", [P, P])
        mean_w = sb("mean_w", [P, P])
        power = sb("power", [P, 8])
        halfpi = sb("halfpi", [P, 1])
        restart = sb("restart", [P, 2 * HALF])
        w_nat = sb("w_nat", [P, 6, 2, D])
        w_flat = w_nat[:, :, :, :].rearrange("p n a d -> p (n a d)")
        whole = w_flat[:, 0:2 * HALF]
        memory = w_flat[:, 2 * HALF:4 * HALF].rearrange("p (n t) -> p n t", n=2)
        turned = w_flat[:, 4 * HALF:6 * HALF].rearrange("p (n t) -> p n t", n=2)
        w_tr = sb("w_tr", [P, 4, 2, D])
        w_kq = sb("w_kq", [P, 2, 2, D])
        wo_g = sb("wo_g", [P, 2, D])
        wo_c = sb("wo_c", [P, 2, D + 1])
        vec_rows = sb("vec_rows", [16, P])
        vec = sb("vec", [P, 8, 2])
        bo_row = sb("bo_row", [1, D])
        wr_nat = sb("wr_nat", [E, D])
        wr_t = sb("wr_t", [P, 2, E])
        kq_bias = sb("kq_bias", [P, 2, 2])
        turns = sb("turns", [P, 2])
        lnb_cols = sb("lnb_cols", [P, 2, P])
        const_row = sb("const_row", [P, D])
        w_qkv = sb("w_qkv", [P, E, 2, QW])

        x_sb = sb("x_sb", [P, 2, TPB, D])
        xn_sb = sb("xn_sb", [P, 2, TPB, GROW])
        base_sb = sb("base_sb", [P, 2, TPB, D])
        xn_t = sb("xn_t", [P, 2, FC, SEQ])
        w_fo = xn_t[:, 0].rearrange("p c t -> p (c t)").rearrange("p (e d) -> p e d", e=E)
        bn = sb("bn", [P, 2, 2, 6])
        mv = sb("mv", [P, 2, 2, 2])
        ve = sb("ve", [P, 2, 2])
        rstd = sb("rstd", [P, 2, 2])
        tanhs = sb("tanhs", [P, 2, 2, HALF])
        frac = sb("frac", [P, 2, 2, HALF])
        frac_abs = sb("frac_abs", [P, 2, HALF])
        trig = sb("trig", [P, 2, 2, 2, HALF])
        bound = sb("bound", [P, 2, HALF])
        retr = sb("retr", [P, 2, FC, HALF])
        retr_sq = sb("retr_sq", [P, 2, FC, HALF])
        proj = sb("proj", [P, 2, TPH, D + 2])
        m_sq = sb("m_sq", [P, TPH])
        var2 = sb("var2", [P, TPH])
        var2e = sb("var2e", [P, 2, TPH])
        rstd2 = sb("rstd2", [P, 2, TPH])
        lg_sb = sb("lg_sb", [E, 2, HALF])

        lg = x_sb[:, 0, 0:4, :].rearrange("p t d -> p (t d)")
        gate = x_sb[:, 0, 4:8, :].rearrange("p t d -> p (t d)")
        gate2 = x_sb[:, 1, 0:4, :].rearrange("p t d -> p (t d)")
        rank_key = x_sb[:, 1, 4:8, :].rearrange("p t d -> p (t d)")
        back_i = base_sb[:, 0, 0:4, :].rearrange("p t d -> p (t d)").bitcast(I32)
        back = base_sb[:, 0, 4:8, :].rearrange("p t d -> p (t d)")
        top8 = sb("top8", [P, 2, 8])
        picked = sb("picked", [P, K])
        row_base = sb("row_base", [P, EXPERT_UNITS], I32)
        row_ids = sb("row_ids", [P, EXPERT_UNITS], I32)

        trig_flat = trig[:, :, :, :, :].rearrange("p s c n t -> p (s c n t)")
        tanh_flat = tanhs[:, :, :, :].rearrange("p s n t -> p (s n t)")
        xg = trig_flat[:, 0:4 * GROW].rearrange("p (s w) -> p s w", s=4)
        xp = trig_flat[:, 4 * GROW:4 * GROW + 4 * D].rearrange("p (s w) -> p s w", s=4)
        xg_t = trig_flat[:, 3072:3584].rearrange("p (s c k) -> p s c k", s=2, c=2)
        qkv = retr_sq[:, :, :, :].rearrange("p s c t -> p (s c t)")[:, 0:4 * QW].rearrange("p (s w) -> p s w", s=4)
        qk_t = tanh_flat[:, 512:1024].rearrange("p (s n w) -> p s n w", s=2, n=2)
        probs = tanh_flat[:, 1024:1280].rearrange("p (s w) -> p s w", s=2)
        probs_t = tanh_flat[:, 1280:1536].rearrange("p (s w) -> p s w", s=2)
        av_t = tanh_flat[:, 1536:1792].rearrange("p (s w) -> p s w", s=2)
        ids_in = sb("ids_in", [P, 4], I32)
        ids_out = sb("ids_out", [P, 4], I32)
        turn_a = sb("turn_a", [P, 2, 2, 2, RH])
        turn_b = sb("turn_b", [P, 2, 2, 2, RH])
        neg_max = sb("neg_max", [P, 2])
        scratch_s = sb("scratch_s", [P, K])
        row_sum = sb("row_sum", [P, 4])
        gate_e = sb("gate_e", [P, 4])
        denom = sb("denom", [P, 1])
        row_scale = sb("row_scale", [P, 2])

        ps = [ctx.enter_context(nc.psum_tensor(f"bank{i}", [P, 512], F32)) for i in range(8)]

        w_in, vec_in, bo_in, wr_in, rope_in, ffn_in, wfo_in = [sem(n) for n in
            ("w_in", "vec_in", "bo_in", "wr_in", "rope_in", "ffn_in", "wfo_in")]
        pool_set, dve_set = sem("pool_set"), sem("dve_set")
        dve_passed, pool_passed = sem("dve_passed"), sem("pool_passed")
        wt_mm, wt_done, vec_mm, vec_done, fold_mm, fold_done = [sem(n) for n in
            ("wt_mm", "wt_done", "vec_mm", "vec_done", "fold_mm", "fold_done")]
        x_in = [sem("x_in0"), sem("x_in1")]
        xn_out = [sem("xn_out0"), sem("xn_out1")]
        lg_out = [sem("lg_out0"), sem("lg_out1")]
        out_out = [sem("out_out0"), sem("out_out1")]
        (bn_done, mv_done, ve_done, rstd_done, xn_done, tp_mm, xnt_done, lg_mm, lg_copied, k_mm, q_mm, v_mm,
         tanh_done, whole_done, frac_done, abs_done, trig_done, bound_done, memory_done, turned_done, retr_done,
         square_done, proj_mm, proj_done, msq_done, var_done, var2e_done, rstd2_done, final_done, base1_done,
         base_done) = [sem(n) for n in (
            "bn_done", "mv_done", "ve_done", "rstd_done", "xn_done", "tp_mm", "xnt_done", "lg_mm", "lg_copied",
            "k_mm", "q_mm", "v_mm", "tanh_done", "whole_done", "frac_done", "abs_done", "trig_done", "bound_done",
            "memory_done", "turned_done", "retr_done", "square_done", "proj_mm", "proj_done", "msq_done",
            "var_done", "var2e_done", "rstd2_done", "final_done", "base1_done", "base_done")]
        lg_in, exp_done, gate_step, top_step, ids_mm, ids_done, row_base_set = [sem(n) for n in (
            "lg_in", "exp_done", "gate_step", "top_step", "ids_mm", "ids_done", "row_base_set")]
        gathered = [sem(f"gathered{i}") for i in range(4)]
        scattered = [sem(f"scattered{i}") for i in range(4)]
        (ids_in_set, ids_out_set, xg_mm, xgt_done, qkv_mm, turn_done, rope_done, qkv_done,
         gate_done, qkt_mm, qkt_done, score_mm, max_done, prob_done, probt_mm, probt_done, av_mm,
         av_done, xp_mm, denom_done, scale_done, xp_done) = [sem(n) for n in (
            "ids_in_set", "ids_out_set", "xg_mm", "xgt_done", "qkv_mm", "turn_done", "rope_done",
            "qkv_done", "gate_done", "qkt_mm", "qkt_done", "score_mm", "max_done", "prob_done",
            "probt_mm", "probt_done", "av_mm", "av_done", "xp_mm", "denom_done", "scale_done", "xp_done")]

        block = ctx.enter_context(nc.Block())

        def wait(eng, s, count):
            if not isinstance(count, int) or count > 0:
                eng.wait_ge(s, count)

        def settle(eng, passed):
            eng.sem_inc(passed, 1)

        def run_steps(eng, step):
            for s in range(-4, 8):
                step(s // 8, s % 8, s)
            with eng.Fori(1, UNITS // 8 - 1) as k:
                for m in range(8):
                    step(k, m, None)
            for s in range(UNITS - 8, UNITS + 5):
                step(s // 8, s % 8, s)

        def has(s, lo, hi):
            return s is None or lo <= s < hi

        def run_expert_steps(eng, step):
            for i in range(-3, 4):
                step(i // 4, i % 4, i)
            with eng.Fori(1, EXPERT_UNITS // 4 - 1) as k:
                for m in range(4):
                    step(k, m, None)
            for i in range(EXPERT_UNITS - 4, EXPERT_UNITS + 3):
                step(i // 4, i % 4, i)

        x_tiles = x.rearrange("b (t p) d -> b p t d", p=P)
        out_tiles = out.rearrange("b (t p) d -> b p t d", p=P)
        out_rows = out.rearrange("b t d -> (b t) d")
        xn_tiles = xn_rows.rearrange("(b t p) d -> b p t d", b=NB, p=P)

        @block.sync
        def _(sp):
            sp.dma_start(x_sb[:, 0], x_tiles[0]).then_inc(x_in[0], 16)
            for n, w in enumerate((Wk, Wq, Wkp, Wqp, Wv, Wo)):
                sp.dma_start(w_nat[:, n], w.rearrange("(a p) d -> p a d", p=P)).then_inc(w_in, 16)
            for n, v in enumerate((bk, bq, bkp, bqp, bv, phase_scale, ln_g, ln_b)):
                sp.dma_start(vec_rows[2 * n:2 * n + 2, :], v.rearrange("(a p) -> a p", p=P)).then_inc(vec_in, 16)
            sp.dma_start(bo_row[:, :], bo.rearrange("(a n) -> a n", a=1)).then_inc(bo_in, 16)
            sp.dma_start(wr_nat[:, :], Wr).then_inc(wr_in, 16)
            for slot in range(2):
                sp.dma_start(xn_sb[:, slot, :, D:GROW], rope.rearrange("(t p) d -> p t d", p=P)
                             ).then_inc(rope_in, 16)
            sp.dma_start(x_sb[:, 1], x_tiles[1]).then_inc(x_in[1], 16)
            for e in range(E):
                sp.dma_start(w_qkv[:, e, :, 0:3 * HP], Wqkv[e].rearrange("(h p) j -> p h j", p=P)
                             ).then_inc(ffn_in, 16)

            def step(k, m, s):
                b = 2 * k + m // 4
                slot = (m // 4) % 2
                if m % 4 == 1 and has(s, 0, UNITS):
                    sp.wait_ge(xn_done, 8 * b + 8)
                    if s is not None and s < 4:
                        sp.wait_ge(rope_in, 32)
                    sp.dma_start(xn_tiles[b], xn_sb[:, slot]).then_inc(xn_out[slot], 16)
                if m % 4 in (2, 3) and has(s, -1, UNITS - 1):
                    half, lb = (1, b) if m % 4 == 2 else (0, b + 1)
                    sp.wait_ge(lg_copied, 2 * lb + half + 1)
                    sp.dma_start(logit_rows[lb][:, half * HALF:(half + 1) * HALF], lg_sb[:, half, :]
                                 ).then_inc(lg_out[half], 16)
                if m % 4 == 3 and has(s, 0, UNITS - 8):
                    sp.wait_ge(base1_done, b + 1)
                    sp.dma_start(x_sb[:, slot], x_tiles[b + 2]).then_inc(x_in[slot], 16)
                if m % 2 == 0 and has(s, 6, UNITS + 6):
                    h_b, j = 2 * k + (m - 6) // 4, ((m - 6) // 2) % 2
                    sp.wait_ge(final_done, 4 * (4 * k + (m - 6) // 2) + 4)
                    sp.dma_start(out_tiles[h_b][:, TPH * j:TPH * j + TPH, :],
                                 base_sb[:, h_b % 2 if s is not None else ((m - 6) // 4) % 2,
                                         TPH * j:TPH * j + TPH, :]).then_inc(out_out[j], 16)

            run_steps(sp, step)
            for half in range(2):
                sp.wait_ge(lg_out[half], 16 * NB)
            sp.wait_ge(base_done, NB)
            sp.wait_ge(v_mm, UNITS)
            sp.wait_ge(lg_mm, 2 * NB)
            sp.dma_start(lg, logit_rows.rearrange("b e t -> (b e) t")).then_inc(lg_in, 16)
            sp.dma_start(w_fo, Wfo.rearrange("e j d -> j e d")).then_inc(wfo_in, 16)
            for j in range(2):
                sp.wait_ge(out_out[j], 16 * NB)
                sp.wait_ge(xn_out[j], 16 * NB // 2)

        @block.tensor
        def _(pe):
            pe.wait_ge(pool_set, 4)
            pe.wait_ge(w_in, 16 * 6)
            for n in range(4):
                for a in range(2):
                    for c in range(2):
                        mm = pe.transpose(ps[n][:, c * D + a * P:c * D + (a + 1) * P],
                                          w_nat[:, 2 + n, a, c * P:(c + 1) * P], ident[:, :])
                mm.then_inc(wt_mm, 1)
            pe.wait_ge(vec_in, 16 * 8)
            pe.transpose(ps[4][:, 0:16], vec_rows[:, :], ident[0:16, 0:16]).then_inc(vec_mm, 1)
            pe.wait_ge(wr_in, 16)
            for c in range(2):
                mm = pe.transpose(ps[5][:, c * E:(c + 1) * E], wr_nat[:, c * P:(c + 1) * P], ident[0:E, 0:E])
            mm.then_inc(vec_mm, 1)
            pe.wait_ge(wt_done, 4)
            pe.wait_ge(vec_done, 2)
            for n in range(2):
                for c in range(2):
                    for a in range(2):
                        mm = pe.matmul(ps[n][:, c * D:(c + 1) * D], w_nat[:, n, a, c * P:(c + 1) * P],
                                       w_tr[:, n, a, :], start=(a == 0), stop=(a == 1))
                mm.then_inc(fold_mm, 1)
            for n in range(2):
                for c in range(2):
                    for a in range(2):
                        mm = pe.matmul(ps[2][:, 2 * n + c:2 * n + c + 1], w_tr[:, n, a, c * P:(c + 1) * P],
                                       vec[:, n, a:a + 1], start=(a == 0), stop=(a == 1))
            mm.then_inc(fold_mm, 1)
            pe.wait_ge(dve_set, 6)
            for c in range(2):
                mm = pe.matmul(ps[3][:, 0:D], mean_w[:, :], wo_g[:, c, :], start=(c == 0), stop=(c == 1))
            mm.then_inc(fold_mm, 1)
            pe.wait_ge(bo_in, 16)
            for c in range(2):
                pe.matmul(ps[6][:, 0:D], lnb_cols[:, c, :], w_tr[:, 3, c, :], start=(c == 0), stop=False)
            pe.matmul(ps[6][:, 0:D], ones[0:1, :], bo_row[:, :], start=False, stop=True).then_inc(fold_mm, 1)
            pe.wait_ge(fold_done, 5)

            K_BANK, Q_BANK, TP_BANK, LG_BANK = ps[0], ps[1], ps[4], ps[5]

            def step(k, m, s):
                u = 8 * k + m
                b = 2 * k + m // 4
                j, f = (m // 2) % 2, m % 2
                slot = (m // 4) % 2
                if has(s, 0, UNITS):
                    rhs = [xn_t[:, slot, c, j * HALF:(j + 1) * HALF] for c in range(2)]
                    wait(pe, xnt_done, 4 * b + 2 * j + 2)
                    for n, (bank, ready) in enumerate(((K_BANK, k_mm), (Q_BANK, q_mm))):
                        wait(pe, tanh_done, 2 * u - 1 + n)
                        for c in range(2):
                            mm = pe.matmul(bank[:, :], w_kq[:, n, c, f * P:(f + 1) * P], rhs[c],
                                           start=(c == 0), stop=(c == 1))
                        mm.then_inc(ready, 1)
                    wait(pe, bound_done, u - 1)
                    for c in range(2):
                        mm = pe.matmul(ps[2 + m % 2][:, :], w_tr[:, 2, c, f * P:(f + 1) * P], rhs[c],
                                       start=(c == 0), stop=(c == 1))
                    mm.then_inc(v_mm, 1)
                if has(s, -3, PAIRS + 1):
                    q, mq = u - 1, (m - 1) % 8
                    wait(pe, xn_done, 2 * q + 10)
                    wait(pe, xnt_done, q + 4)
                    for t in range(2):
                        for c in range(2):
                            mm = pe.transpose(TP_BANK[:, c * D + t * P:c * D + (t + 1) * P],
                                              xn_sb[:, (mq // 4 + 1) % 2, 2 * (mq % 4) + t, c * P:(c + 1) * P],
                                              ident[:, :])
                    mm.then_inc(tp_mm, 1)
                first = m % 2 == 1
                if has(s, 3, UNITS + 3):
                    h, mh = 4 * k + (m - (3 if first else 4)) // 2, ((m - (3 if first else 4)) // 2) % 2
                    wait(pe, retr_done, 2 * h + 2)
                    wait(pe, square_done, 2 * h + 2)
                    for t in range(0, 2) if first else range(2, 4):
                        bank = ps[6 + t % 2]
                        wait(pe, proj_done, 4 * h + t - 1)
                        for c in range(2):
                            pe.matmul(bank[:, 0:D + 1], retr[:, mh, c, t * P:(t + 1) * P], wo_c[:, c, :],
                                      start=(c == 0), stop=(c == 1))
                        for c in range(2):
                            mm = pe.matmul(bank[:, D + 1:D + 2], retr_sq[:, mh, c, t * P:(t + 1) * P],
                                           ones[:, 0:1], start=(c == 0), stop=(c == 1))
                        mm.then_inc(proj_mm, 1)
                if m % 4 in (1, 2) and has(s, -2, UNITS - 2):
                    half, lb = (1, b) if m % 4 == 1 else (0, b + 1)
                    lslot = slot if half else 1 - slot
                    wait(pe, xnt_done, 4 * lb + 2 * half + 2)
                    wait(pe, lg_copied, 2 * lb + half)
                    for c in range(2):
                        mm = pe.matmul(LG_BANK[0:E, :], wr_t[:, c, :],
                                       xn_t[:, lslot, c, half * HALF:(half + 1) * HALF],
                                       start=(c == 0), stop=(c == 1))
                    mm.then_inc(lg_mm, 1)

            run_steps(pe, step)

            pe.wait_ge(top_step, 64)
            pe.wait_ge(lg_copied, 2 * NB)
            pe.wait_ge(proj_done, 4 * HALVES)
            pe.transpose(ps[0][:, 0:P], picked[:, :], ident[:, :]).then_inc(ids_mm, 1)
            pe.wait_ge(ids_done, 1)
            pe.wait_ge(wfo_in, 16)

            def expert_step(k, m, i):
                n = 4 * k + m
                if has(i, 0, EXPERT_UNITS):
                    wait(pe, xgt_done, n + 1)
                    for c in range(2):
                        mm = pe.matmul(ps[1][:, 0:QW], xg_t[:, m % 2, c, :], w_qkv[:, k // 4, c, :],
                                       start=(c == 0), stop=(c == 1))
                    mm.then_inc(qkv_mm, 1)
                if has(i, -1, EXPERT_UNITS - 1):
                    g = (m + 1) % 4
                    pe.wait_ge(gathered[g], 16 * (k + (m + 1) // 4) + 16)
                    for c in range(2):
                        mm = pe.transpose(ps[0][:, c * P:(c + 1) * P], xg[:, g, c * P:(c + 1) * P], ident[:, :])
                    mm.then_inc(xg_mm, 1)
                if has(i, 1, EXPERT_UNITS + 1):
                    wait(pe, rope_done, n)
                    for t in range(2):
                        mm = pe.transpose(ps[2][:, t * K:(t + 1) * K], qkv[:, (m - 1) % 4, t * HP:(t + 1) * HP],
                                          ident[:, :])
                    mm.then_inc(qkt_mm, 1)
                if has(i, 2, EXPERT_UNITS + 2):
                    wait(pe, prob_done, n - 1)
                    pe.transpose(ps[4][:, 0:K], probs[:, m % 2, :], ident[:, :]).then_inc(probt_mm, 1)
                if has(i, 3, EXPERT_UNITS + 3):
                    wait(pe, av_done, n - 2)
                    if i is not None and i > EXPERT_UNITS:
                        wait(pe, xp_done, n - 4)
                    pe.matmul(ps[6 + (m - 3) % 2][:, 0:D], av_t[:, (m - 3) % 2, :],
                              w_fo[:, (k + (m - 3) // 4) // 4, :], start=True, stop=True).then_inc(xp_mm, 1)
                if has(i, 1, EXPERT_UNITS + 1):
                    u = (m - 1) % 2
                    wait(pe, qkt_done, n)
                    pe.matmul(ps[3][:, 0:K], qk_t[:, u, 0, :], qk_t[:, u, 1, :], start=True, stop=False)
                    pe.matmul(ps[3][:, 0:K], ident_bf[:, :], causal[:, :], start=False, stop=True
                              ).then_inc(score_mm, 1)
                if has(i, 2, EXPERT_UNITS + 2):
                    wait(pe, probt_done, n - 1)
                    pe.matmul(ps[5][:, 0:K], qkv[:, (m - 2) % 4, 2 * HP:3 * HP], probs_t[:, m % 2, :],
                              start=True, stop=True).then_inc(av_mm, 1)

            run_expert_steps(pe, expert_step)

        @block.scalar
        def _(act):
            nc.scalar.preload_act_table_set("silu_and_others")
            for n in range(4):
                act.wait_ge(wt_mm, n + 1)
                nc.scalar.activation(w_tr[:, n], ps[n][:, :].rearrange("p (c d) -> p c d", c=2), ACT.Copy
                                     ).then_inc(wt_done, 1)
            act.wait_ge(vec_mm, 1)
            nc.scalar.activation(vec[:, :, :], ps[4][:, 0:16].rearrange("p (n a) -> p n a", a=2), ACT.Copy
                                 ).then_inc(vec_done, 1)
            act.wait_ge(vec_mm, 2)
            nc.scalar.activation(wr_t[:, :, :], ps[5][:, 0:2 * E].rearrange("p (c e) -> p c e", c=2), ACT.Copy
                                 ).then_inc(vec_done, 1)
            for n in range(2):
                act.wait_ge(fold_mm, n + 1)
                nc.scalar.activation(w_kq[:, n], ps[n][:, :].rearrange("p (c d) -> p c d", c=2), ACT.Copy
                                     ).then_inc(fold_done, 1)

            def step(k, m, s):
                u = 8 * k + m
                b = 2 * k + m // 4
                f, slot = m % 2, (m // 4) % 2
                if has(s, 0, UNITS):
                    wait(act, frac_done, u - 1)
                    for n, (bank, ready) in enumerate(((ps[0], k_mm), (ps[1], q_mm))):
                        act.wait_ge(ready, u + 1)
                        nc.scalar.activation(tanhs[:, m % 2, n, :], bank[:, :], ACT.Tanh,
                                             bias=kq_bias[:, n, f:f + 1]).then_inc(tanh_done, 1)
                if has(s, 2, UNITS + 2):
                    wait(act, retr_done, u - 1)
                    wait(act, proj_mm, 4 * (4 * k + (m - 2) // 2) - 4)
                    r = ((m - 2) // 2) % 2
                    nc.scalar.activation(retr_sq[:, r, f, :], retr[:, r, f, :], ACT.Square
                                         ).then_inc(square_done, 1)
                if has(s, -3, PAIRS + 1):
                    q, mq = u - 1, (m - 1) % 8
                    wait(act, tp_mm, q + 5)
                    qslot = (mq // 4 + 1) % 2
                    wait(act, v_mm, 4 * (2 * k + (m - 1) // 4))
                    wait(act, lg_mm, 2 * (2 * k + (m - 1) // 4))
                    nc.scalar.activation(xn_t[:, qslot, :, (mq % 4) * D:(mq % 4 + 1) * D],
                                         ps[4][:, :].rearrange("p (c d) -> p c d", c=2), ACT.Copy
                                         ).then_inc(xnt_done, 1)
                if has(s, 0, UNITS):
                    act.wait_ge(frac_done, u + 1)
                    wait(act, turned_done, u - 1)
                    nc.scalar.activation(frac_abs[:, :, :], frac[:, m % 2], ACT.Abs).then_inc(abs_done, 1)
                    nc.scalar.activation(trig[:, m % 2, 1], frac[:, m % 2], ACT.Sin, scale=TWO_PI
                                         ).then_inc(trig_done, 1)
                    act.wait_ge(abs_done, u + 1)
                    nc.scalar.activation(trig[:, m % 2, 0], frac_abs[:, :, :], ACT.Sin, scale=-TWO_PI,
                                         bias=halfpi[:, 0:1]).then_inc(trig_done, 1)
                first = m % 2 == 1
                if has(s, 3, UNITS + 3):
                    h, mh = 4 * k + (m - (3 if first else 4)) // 2, ((m - (3 if first else 4)) // 2) % 2
                    wait(act, final_done, 4 * h - 4)
                    for t in range(0, 2) if first else range(2, 4):
                        wait(act, proj_mm, 4 * h + t + 1)
                        nc.scalar.activation(proj[:, mh, t, :], ps[6 + t % 2][:, 0:D + 2], ACT.Copy
                                             ).then_inc(proj_done, 1)
                if m % 4 in (1, 2) and has(s, -2, UNITS - 2):
                    half, lb = (1, b) if m % 4 == 1 else (0, b + 1)
                    wait(act, lg_mm, 2 * lb + half + 1)
                    wait(act, lg_out[half], 16 * lb)
                    nc.scalar.activation(lg_sb[:, half, :], ps[5][0:E, :], ACT.Copy
                                         ).then_inc(lg_copied, 1)

            run_steps(act, step)
            nc.scalar.preload_act_table_set("exp_and_others")
            act.wait_ge(lg_in, 16)
            nc.scalar.activation(gate, lg, ACT.Exp, scale=-1.0).then_inc(exp_done, 1)

            def expert_step(k, m, i):
                n = 4 * k + m
                if has(i, 0, EXPERT_UNITS):
                    wait(act, qkv_mm, n + 1)
                    nc.scalar.activation(qkv[:, m, :], ps[1][:, 0:QW], ACT.Copy).then_inc(qkv_done, 1)
                if has(i, -1, EXPERT_UNITS - 1):
                    wait(act, xg_mm, n + 2)
                    nc.scalar.activation(xg_t[:, (m + 1) % 2], ps[0][:, 0:D].rearrange("p (c k) -> p c k", c=2),
                                         ACT.Copy).then_inc(xgt_done, 1)
                if has(i, 1, EXPERT_UNITS + 1):
                    wait(act, qkt_mm, n)
                    nc.scalar.activation(qk_t[:, (m - 1) % 2], ps[2][:, 0:2 * K].rearrange("p (t k) -> p t k", t=2),
                                         ACT.Copy).then_inc(qkt_done, 1)
                if has(i, 2, EXPERT_UNITS + 2):
                    wait(act, probt_mm, n - 1)
                    nc.scalar.activation(probs_t[:, m % 2, :], ps[4][:, 0:K], ACT.Copy).then_inc(probt_done, 1)
                if has(i, 1, EXPERT_UNITS + 1):
                    mp = (m - 1) % 4
                    wait(act, max_done, n)
                    nc.scalar.activation(probs[:, mp % 2, :], ps[3][:, 0:K], ACT.Exp, scale=SCALE,
                                         bias=neg_max[:, mp % 2:mp % 2 + 1], accum_out=row_sum[:, mp:mp + 1]
                                         ).then_inc(prob_done, 1)
                    wait(act, qkv_done, n)
                    nc.scalar.activation(gate_e[:, mp:mp + 1], qkv[:, mp, 3 * HP:QW], ACT.Exp, scale=-1.0
                                         ).then_inc(gate_done, 1)
                if has(i, 2, EXPERT_UNITS + 2):
                    wait(act, av_mm, n - 1)
                    nc.scalar.activation(av_t[:, m % 2, :], ps[5][:, 0:K], ACT.Copy).then_inc(av_done, 1)

            act.wait_ge(ids_done, 1)
            run_expert_steps(act, expert_step)

        @block.vector
        def _(dve):
            nc.vector.memset(ones[:, :], 1.0).then_inc(dve_set, 1)
            nc.vector.memset(mean_w[:, :], 1.0 / D).then_inc(dve_set, 1)
            nc.vector.memset(halfpi[:, :], float(np.pi / 2))
            nc.vector.memset(power[:, :], -0.5)
            nc.vector.memset(restart[:, :], 1.0).then_inc(bn_done, 1)
            nc.vector.memset(wo_c[:, :, D:D + 1], 1.0)
            dve.wait_ge(bn_done, 1)
            nc.vector.memset(restart[:, :].rearrange("p (n c) -> p n c", c=CH)[:, :, 0:1], 0.0
                             ).then_inc(bn_done, 1)
            dve.wait_ge(vec_done, 1)
            dve.wait_ge(wt_done, 4)
            dve.wait_ge(dve_set, 2)
            for c in range(2):
                nc.vector.tensor_scalar(wo_g[:, c, :], w_tr[:, 3, c, :], vec[:, 6, c:c + 1], None, ALU.mult
                                        ).then_inc(dve_set, 1)
            nc.vector.tensor_scalar(turns[:, :], vec[:, 5, :], 1.0 / TWO_PI, None, ALU.mult)
            for c in range(2):
                nc.vector.tensor_scalar(lnb_cols[:, c, :], ones[:, :], vec[:, 7, c:c + 1], None, ALU.mult
                                        ).then_inc(dve_set, 1)
            dve.wait_ge(vec_done, 2)
            dve.wait_ge(ffn_in, 16 * E)
            nc.vector.tensor_copy(w_qkv[:, :, :, 3 * HP:QW].rearrange("p e c o -> p e (c o)"),
                                  wr_t[:, :, :].rearrange("p c e -> p e c"))
            dve.wait_ge(fold_mm, 3)
            nc.vector.tensor_tensor(kq_bias[:, :, :], ps[2][:, 0:4].rearrange("p (n c) -> p n c", n=2),
                                    vec[:, 2:4, :], ALU.add).then_inc(fold_done, 1)
            dve.wait_ge(fold_mm, 4)
            nc.vector.tensor_tensor(wo_c[:, :, 0:D], wo_g[:, :, :],
                                    ps[3][:, 0:D].unsqueeze(1).to_broadcast([P, 2, D]), ALU.subtract
                                    ).then_inc(fold_done, 1)
            dve.wait_ge(fold_mm, 5)
            nc.vector.tensor_copy(const_row[:, :], ps[6][:, 0:D]).then_inc(fold_done, 1)
            dve.wait_ge(fold_done, 5)

            BN0 = 2

            def step(k, m, s):
                u = 8 * k + m
                f = m % 2
                if has(s, -3, PAIRS + 1):
                    q, mq = u - 1, (m - 1) % 8
                    slot = (mq // 4 + 1) % 2
                    wait(dve, rstd_done, q + 5)
                    if mq % 4 == 0:
                        wait(dve, xn_out[slot], 16 * (k + ((m - 1) // 4 + 1) // 2))
                        wait(dve, base1_done, 2 * k + (m - 1) // 4)
                    for t in range(2):
                        nc.vector.tensor_scalar(xn_sb[:, slot, 2 * (mq % 4) + t, 0:D],
                                                x_sb[:, slot, 2 * (mq % 4) + t, :],
                                                mv[:, mq % 2, t, 0:1], rstd[:, mq % 2, t:t + 1],
                                                ALU.subtract, ALU.mult).then_inc(xn_done, 1)
                if has(s, 0, UNITS):
                    wait(dve, tanh_done, 2 * u + 2)
                    both = tanhs[:, m % 2].rearrange("p n t -> p (n t)")
                    nc.vector.tensor_scalar(whole[:, :], both, turns[:, f:f + 1], ROUND, ALU.mult, ALU.add
                                            ).then_inc(whole_done, 1)
                    dve.wait_ge(whole_done, u + 1)
                    wait(dve, trig_done, 2 * u - 2)
                    nc.vector.scalar_tensor_tensor(
                        out=frac[:, m % 2].rearrange("p n t -> p (n t)"), in0=both, scalar=turns[:, f:f + 1],
                        in1=whole[:, :].bitcast(I16).rearrange("p (t w) -> p t w", w=2)[:, :, 0],
                        op0=ALU.mult, op1=ALU.subtract).then_inc(frac_done, 1)
                if has(s, -4, PAIRS):
                    slot = (m // 4 + 1) % 2
                    wait(dve, x_in[slot], 16 * (k + (m // 4 + 1) // 2) + 16)
                    for t in range(2):
                        nc.vector.bn_stats(bn[:, m % 2, t, :], x_sb[:, slot, 2 * (m % 4) + t, :]
                                           ).then_inc(bn_done, 1)
                    for t in range(2):
                        dve.wait_ge(bn_done, BN0 + 2 * u + 9 + t)
                        settle(dve, dve_passed)
                        nc.vector.bn_aggr(mv[:, m % 2, t, :], bn[:, m % 2, t, :]).then_inc(mv_done, 1)
                    dve.wait_ge(mv_done, 2 * u + 10)
                    wait(dve, rstd_done, u + 3)
                    nc.vector.tensor_scalar(ve[:, m % 2, :], mv[:, m % 2, :, 1], EPS, None, ALU.add
                                            ).then_inc(ve_done, 1)
                if has(s, 1, UNITS + 1):
                    p = (m - 1) % 2
                    fp = (m - 1) % 2
                    wait(dve, v_mm, u)
                    wait(dve, trig_done, 2 * u)
                    nc.vector.scalar_tensor_tensor(
                        out=bound[:, :, :], in0=ps[2 + p][:, :].unsqueeze(1).to_broadcast([P, 2, HALF]),
                        scalar=vec[:, 4, fp:fp + 1], in1=trig[:, p, :, 0, :], op0=ALU.add, op1=ALU.mult
                    ).then_inc(bound_done, 1)
                    wait(dve, bound_done, u)
                    nc.vector.tensor_tensor_scan(memory[:, :, :].rearrange("p n t -> p (n t)"), restart[:, :],
                                                 bound[:, :, :].rearrange("p n t -> p (n t)"), 0.0,
                                                 ALU.mult, ALU.add).then_inc(memory_done, 1)
                    wait(dve, memory_done, u)
                    nc.vector.tensor_tensor(turned[:, :, :], memory[:, :, :], trig[:, p, :, 1, :], ALU.mult
                                            ).then_inc(turned_done, 1)
                    wait(dve, turned_done, u)
                    mr = ((m - 1) // 2) % 2
                    wait(dve, proj_mm, 4 * (4 * k + (m - 1) // 2) - 4)
                    nc.vector.tensor_tensor(retr[:, mr, fp, :], turned[:, 0, :], turned[:, 1, :], ALU.add
                                            ).then_inc(retr_done, 1)
                if m % 2 == 1 and has(s, 5, UNITS + 4):
                    h, mh = 4 * k + (m - 5) // 2, ((m - 5) // 2) % 2
                    wait(dve, proj_done, 4 * h + 4)
                    total, total_sq = proj[:, mh, :, D], proj[:, mh, :, D + 1]
                    nc.vector.scalar_tensor_tensor(out=m_sq[:, :], in0=total, scalar=1.0 / (D * D), in1=total,
                                                   op0=ALU.mult, op1=ALU.mult).then_inc(msq_done, 1)
                    wait(dve, msq_done, h + 1)
                    nc.vector.scalar_tensor_tensor(out=var2[:, :], in0=total_sq, scalar=1.0 / D, in1=m_sq[:, :],
                                                   op0=ALU.mult, op1=ALU.subtract).then_inc(var_done, 1)
                    wait(dve, var_done, h + 1)
                    wait(dve, rstd2_done, h - 1)
                    nc.vector.tensor_scalar(var2e[:, mh, :], var2[:, :], 0.0, EPS * D, ALU.max, ALU.add
                                            ).then_inc(var2e_done, 1)
                if m % 2 == 0 and has(s, 6, UNITS + 5):
                    h, mh = 4 * k + (m - 6) // 2, ((m - 6) // 2) % 2
                    slot, j = ((m - 6) // 4) % 2, ((m - 6) // 2) % 2
                    wait(dve, rstd2_done, h + 1)
                    wait(dve, base_done, 2 * k + (m - 6) // 4 + 1)
                    for t in range(TPH):
                        row = base_sb[:, slot, TPH * j + t, :]
                        nc.vector.scalar_tensor_tensor(out=row, in0=proj[:, mh, t, 0:D],
                                                       scalar=rstd2[:, mh, t:t + 1], in1=row,
                                                       op0=ALU.mult, op1=ALU.add).then_inc(final_done, 1)

            run_steps(dve, step)

            dve.wait_ge(exp_done, 1)
            nc.vector.tensor_scalar(gate, gate, 1.0, None, ALU.add).then_inc(gate_step, 1)
            dve.wait_ge(gate_step, 1)
            nc.vector.reciprocal(gate2, gate).then_inc(gate_step, 1)
            dve.wait_ge(gate_step, 2)
            steps = 0

            def top_rounds(values, replaced_by, keep):
                nonlocal steps
                for r in range(K // 8):
                    eight = picked[:, 8 * r:8 * r + 8] if keep else top8[:, r % 2, :]
                    nc.vector.max(eight, values).then_inc(top_step, 1)
                    steps += 1
                    dve.wait_ge(top_step, steps)
                    nc.vector.match_replace(values, eight, values, replaced_by).then_inc(top_step, 1)
                    steps += 1
                    dve.wait_ge(top_step, steps)

            top_rounds(gate2, -1.0, False)
            dve.wait_ge(row_base_set, 2)
            nc.vector.tensor_copy(back, back_i).then_inc(gate_step, 1)
            dve.wait_ge(gate_step, 3)
            nc.vector.scalar_tensor_tensor(out=rank_key, in0=gate2, scalar=0.0, in1=back, op0=ALU.is_lt,
                                           op1=ALU.mult).then_inc(gate_step, 1)
            dve.wait_ge(gate_step, 4)
            top_rounds(rank_key, 0.0, True)
            dve.wait_ge(ids_mm, 1)
            by_expert = "p (e b) -> p e b"
            nc.vector.tensor_tensor(row_ids[:, :].rearrange(by_expert, e=E),
                                    row_base[:, :].rearrange(by_expert, e=E),
                                    ps[0][:, 0:P].rearrange("p (b e) -> p e b", e=E), ALU.subtract
                                    ).then_inc(ids_done, 1)

            def expert_step(k, m, i):
                n = 4 * k + m
                if has(i, 0, EXPERT_UNITS):
                    heads = qkv[:, m, 0:2 * HP]
                    rotated = heads.rearrange("p (t h r) -> p t h r", t=2, r=RH)[:, :, 0:2, :]
                    row = xg[:, m, :]
                    cos = row[:, D:D + RH].unsqueeze(1).unsqueeze(1).to_broadcast([P, 2, 2, RH])
                    wait(dve, qkv_done, n + 1)
                    nc.vector.tensor_tensor(turn_a[:, m % 2], rotated, cos, ALU.mult).then_inc(turn_done, 1)
                    for h in range(2):
                        sin = row[:, D + (1 + h) * RH:D + (2 + h) * RH].unsqueeze(1).to_broadcast([P, 2, RH])
                        nc.vector.tensor_tensor(turn_b[:, m % 2, :, h, :], rotated[:, :, 1 - h, :], sin, ALU.mult
                                                ).then_inc(turn_done, 1)
                    dve.wait_ge(turn_done, 3 * n + 3)
                    nc.vector.tensor_tensor(
                        heads.rearrange("p (t j) -> p t j", t=2)[:, :, 0:ROT], turn_a[:, m % 2].rearrange("p t h r -> p t (h r)"),
                        turn_b[:, m % 2].rearrange("p t h r -> p t (h r)"), ALU.add).then_inc(rope_done, 1)
                if has(i, 1, EXPERT_UNITS + 1):
                    u = (m - 1) % 2
                    wait(dve, score_mm, n)
                    nc.vector.tensor_scalar(scratch_s[:, :], ps[3][:, 0:K], -SCALE, None, ALU.mult, ALU.min,
                                            accum_out=neg_max[:, u:u + 1]).then_inc(max_done, 1)
                if has(i, 3, EXPERT_UNITS + 3):
                    u = (m - 3) % 4
                    wait(dve, gate_done, n - 2)
                    nc.vector.scalar_tensor_tensor(out=denom[:, :], in0=gate_e[:, u:u + 1], scalar=1.0,
                                                   in1=row_sum[:, u:u + 1], op0=ALU.add, op1=ALU.mult
                                                   ).then_inc(denom_done, 1)
                    wait(dve, denom_done, n - 2)
                    nc.vector.reciprocal(row_scale[:, u % 2:u % 2 + 1], denom[:, :]).then_inc(scale_done, 1)
                    wait(dve, scattered[u], 16 * (k + (m - 3) // 4))
                    wait(dve, xp_mm, n - 2)
                    wait(dve, scale_done, n - 2)
                    nc.vector.tensor_scalar(xp[:, u, :], ps[6 + u % 2][:, 0:D], row_scale[:, u % 2:u % 2 + 1], None,
                                            ALU.mult).then_inc(xp_done, 1)

            run_expert_steps(dve, expert_step)

        @block.gpsimd
        def _(pool):
            nc.gpsimd.memset(ident[:, :], 0.0).then_inc(pool_set, 1)
            nc.gpsimd.memset(causal[:, :], 0.0).then_inc(pool_set, 1)
            pool.wait_ge(pool_set, 2)
            nc.gpsimd.affine_select(out=ident[:, :], in_=ident[:, :], compare_op=ALU.not_equal, fill=1.0, base=0,
                                    pattern=[[-1, P]], channel_multiplier=1).then_inc(pool_set, 1)
            nc.gpsimd.affine_select(out=causal[:, :], in_=causal[:, :], compare_op=ALU.is_ge, fill=MASKED, base=0,
                                    pattern=[[-1, K]], channel_multiplier=1).then_inc(pool_set, 1)
            pool.wait_ge(pool_set, 4)
            nc.gpsimd.tensor_copy(ident_bf[:, :], ident[:, :]).then_inc(pool_set, 1)
            nc.gpsimd.iota(row_base[:, :], pattern=[[0, E], [SEQ, NB]], base=SEQ, channel_multiplier=0
                           ).then_inc(row_base_set, 1)
            pool.wait_ge(bn_done, 2)

            def step(k, m, s):
                u = 8 * k + m
                if has(s, -4, PAIRS):
                    wait(pool, ve_done, u + 5)
                    if not (s is not None and s < -2):
                        wait(pool, xn_done, 2 * u + 6)
                    nc.gpsimd.tensor_tensor(rstd[:, m % 2, :], ve[:, m % 2, :], power[:, 0:2], ALU.pow
                                            ).then_inc(rstd_done, 1)
                if m % 2 == 1 and has(s, 5, UNITS + 4):
                    h, mh = 4 * k + (m - 5) // 2, ((m - 5) // 2) % 2
                    wait(pool, var2e_done, h + 1)
                    wait(pool, final_done, 4 * h - 4)
                    nc.gpsimd.tensor_tensor(rstd2[:, mh, :], var2e[:, mh, :], power[:, 0:TPH], ALU.pow
                                            ).then_inc(rstd2_done, 1)
                if m % 4 == 2 and has(s, 0, UNITS):
                    b, slot = 2 * k + m // 4, (m // 4) % 2
                    wait(pool, xn_done, 8 * b + 8)
                    for j in range(2):
                        wait(pool, out_out[j], 16 * (b - 1))
                    nc.gpsimd.tensor_tensor(base_sb[:, slot], x_sb[:, slot], xn_sb[:, slot, :, 0:D], ALU.add
                                            ).then_inc(base1_done, 1)
                    pool.wait_ge(base1_done, b + 1)
                    if s is not None and s < 4:
                        pool.wait_ge(fold_done, 5)
                    nc.gpsimd.tensor_tensor(base_sb[:, slot], base_sb[:, slot],
                                            const_row[:, :].unsqueeze(1).to_broadcast([P, TPB, D]), ALU.add
                                            ).then_inc(base_done, 1)

            run_steps(pool, step)
            for j in range(2):
                pool.wait_ge(out_out[j], 16 * NB)
                pool.wait_ge(xn_out[j], 16 * NB // 2)
            nc.gpsimd.iota(back_i, pattern=[[-1, SEQ]], base=SEQ, channel_multiplier=0).then_inc(row_base_set, 1)
            pool.wait_ge(ids_done, 1)

            def expert_step(k, m, i):
                n = 4 * k + m
                if has(i, -3, EXPERT_UNITS - 3):
                    g = (m + 3) % 4
                    kg = k + (m + 3) // 4
                    wait(pool, gathered[g], 16 * kg)
                    wait(pool, rope_done, n)
                    wait(pool, xg_mm, n)
                    nc.gpsimd.tensor_copy(ids_in[:, g:g + 1], row_ids[:, bass.ds(n + 3, 1)]
                                          ).then_inc(ids_in_set, 1)
                    pool.wait_ge(ids_in_set, n + 4)
                    settle(pool, pool_passed)
                    nc.gpsimd.indirect_dma_start(
                        out=xg[:, g, :], out_offset=None, in_=xn_rows,
                        in_offset=bass.IndirectOffsetOnAxis(ap=ids_in[:, g:g + 1].bitcast(U32), axis=0)
                    ).then_inc(gathered[g], 16)
                if has(i, 3, EXPERT_UNITS + 3):
                    g = (m - 3) % 4
                    ks = k + (m - 3) // 4
                    wait(pool, scattered[g], 16 * ks)
                    nc.gpsimd.tensor_copy(ids_out[:, g:g + 1], row_ids[:, bass.ds(n - 3, 1)]
                                          ).then_inc(ids_out_set, 1)
                    pool.wait_ge(ids_out_set, n - 2)
                    wait(pool, xp_done, n - 2)
                    settle(pool, pool_passed)
                    nc.gpsimd.indirect_dma_start(
                        out=out_rows, out_offset=bass.IndirectOffsetOnAxis(ap=ids_out[:, g:g + 1].bitcast(U32),
                                                                           axis=0),
                        in_=xp[:, g, :], in_offset=None, compute_op=ALU.add).then_inc(scattered[g], 16)

            run_expert_steps(pool, expert_step)
            for g in range(4):
                pool.wait_ge(scattered[g], 16 * EXPERT_UNITS // 4)


def rope_rows():
    inv_freq = (1.0 / np.float32(10000.0) ** (np.arange(RH, dtype=np.float32) * np.float32(2.0) / np.float32(ROT))
                ).astype(np.float32)
    angle = np.arange(SEQ, dtype=np.float32)[:, None] * inv_freq
    cos, sin = np.cos(angle), np.sin(angle)
    return np.ascontiguousarray(np.concatenate([cos, -sin, sin], axis=1).astype(np.float32))


_INS = ["L0_attn_x", "L0_attn_Wk", "L0_attn_bk", "L0_attn_Wv", "L0_attn_bv", "L0_attn_Wq", "L0_attn_bq",
        "L0_attn_Wkp", "L0_attn_bkp", "L0_attn_Wqp", "L0_attn_bqp", "L0_attn_phase_scale", "L0_attn_ln_g",
        "L0_attn_ln_b", "L0_attn_Wo", "L0_attn_bo", "L0_ffn_Wr", "L0_ffn_Wqkv", "L0_ffn_Wo"]


def kernel(**inputs):
    import concourse.bacc as bacc
    from concourse.bass_utils import run_bass_kernel_spmd

    nc = bacc.Bacc("TRN2", target_bir_lowering=False, num_devices=1)
    arrays, args = {}, []
    for name in _INS:
        a = np.ascontiguousarray(inputs[name])
        arrays[f"in_{name}"] = a
        args.append(nc.dram_tensor(f"in_{name}", a.shape, mybir.dt.from_np(a.dtype), kind="ExternalInput").ap())
    arrays["rope_rows"] = rope_rows()
    args.append(nc.dram_tensor("rope_rows", [SEQ, 3 * RH], F32, kind="ExternalInput").ap())
    args.append(nc.dram_tensor("out_x", [NB, SEQ, D], F32, kind="ExternalOutput").ap())
    build(nc, *args)
    r = run_bass_kernel_spmd(nc, [arrays], core_ids=[0])
    return r.results[0]["out_x"]
```

```python
from contextlib import ExitStack

import numpy as np

import concourse.bass as bass
import concourse.mybir as mybir

F32 = mybir.dt.float32
F32R = mybir.dt.float32r
BF16 = mybir.dt.bfloat16
I32 = mybir.dt.int32
I16 = mybir.dt.int16
U32 = mybir.dt.uint32
ALU = mybir.AluOpType
ACT = mybir.ActivationFunctionType
AX = mybir.AxisListType

P = 128
NB, SEQ, D = 16, 1024, 256
NTOK = NB * SEQ
CH = 64
FC = D // P
HALF = 512
TPH = HALF // P
TPB = SEQ // P
UNITS = NB * (SEQ // HALF) * FC
PAIRS = UNITS - 4
HALVES = UNITS // 2
E, HP, ROT = 8, 128, 64
RH = ROT // 2
K = SEQ // 8
GROW = D + 3 * RH
QW = 3 * HP + 1
EPS = 1e-5
TWO_PI = float(2 * np.pi)
ROUND = float(1.5 * 2 ** 23)
MASKED = -1e30
SCALE = float(HP) ** -0.5
EXPERT_UNITS = NB * E


def build(nc, x, Wk, bk, Wv, bv, Wq, bq, Wkp, bkp, Wqp, bqp, phase_scale, ln_g, ln_b, Wo, bo, Wr, Wqkv, Wfo,
          rope, out):
    with ExitStack() as ctx:
        def sb(name, shape, dt=F32):
            return ctx.enter_context(nc.sbuf_tensor(name, shape, dt))

        def sem(name):
            return ctx.enter_context(nc.semaphore(name))

        xn_rows = nc.dram_tensor("xn_rows", [NTOK, GROW], F32, kind="Internal").ap()
        logit_rows = nc.dram_tensor("logit_rows", [2, NB, E, SEQ], F32, kind="Internal").ap()

        ident = sb("ident", [P, P])
        ident_bf = sb("ident_bf", [P, P], BF16)
        causal = sb("causal", [P, K], BF16)
        ones = sb("ones", [P, P])
        mean_w = sb("mean_w", [P, P])
        power = sb("power", [P, 8])
        halfpi = sb("halfpi", [P, 1])
        restart = sb("restart", [P, 2 * HALF])
        w_nat = sb("w_nat", [P, 6, 2, D])
        w_flat = w_nat[:, :, :, :].rearrange("p n a d -> p (n a d)")
        whole = w_flat[:, 0:2 * HALF]
        memory = w_flat[:, 2 * HALF:4 * HALF].rearrange("p (n t) -> p n t", n=2)
        turned = [w_flat[:, 4 * HALF:6 * HALF].rearrange("p (n t) -> p n t", n=2), sb("turned", [P, 2, HALF])]
        w_tr = sb("w_tr", [P, 4, 2, D])
        xn_stage = w_tr[:, 0:2]
        w_split = sb("w_split", [P, 3, 2, 2, D], F32R)
        wr_split = sb("wr_split", [P, 2, 2, E], F32R)
        wo_g = sb("wo_g", [P, 2, D])
        wo_c = sb("wo_c", [P, 2, D + 1])
        vec_rows = sb("vec_rows", [16, P])
        vec = sb("vec", [P, 8, 2])
        bo_row = sb("bo_row", [1, D])
        wr_nat = sb("wr_nat", [E, D])
        wr_t = sb("wr_t", [P, 2, E])
        kq_bias = sb("kq_bias", [P, 2, 2])
        turns = sb("turns", [P, 2])
        lnb_cols = sb("lnb_cols", [P, 2, P])
        const_row = sb("const_row", [P, D])

        x_sb = sb("x_sb", [P, 2, TPB, D])
        row_area = sb("row_area", [P, max(2 * TPB * GROW, E * 2 * QW)])
        xn_sb = row_area[:, 0:2 * TPB * GROW].rearrange("p (s t w) -> p s t w", s=2, t=TPB)
        w_qkv = row_area[:, 0:E * 2 * QW].rearrange("p (e h j) -> p e h j", e=E, h=2)
        base_sb = sb("base_sb", [P, 2, TPB, D])
        xn_hi = sb("xn_hi", [P, 2, FC, HALF], F32R)
        xn_lo = sb("xn_lo", [P, 2, FC, HALF], F32R)
        bn = sb("bn", [P, 2, 2, 6])
        mv = sb("mv", [P, 2, 2, 2])
        ve = sb("ve", [P, 2, 2])
        neg_mean = sb("neg_mean", [P, 2, 2])
        shift = sb("shift", [P, 2, 2])
        rstd = sb("rstd", [P, 2, 2])
        tanhs = sb("tanhs", [P, 2, 2, HALF])
        frac = sb("frac", [P, 2, 2, HALF])
        w_fo = frac[:, :, :, :].rearrange("p s n t -> p (s n t)").rearrange("p (e d) -> p e d", e=E)
        frac_abs = sb("frac_abs", [P, 2, 2, HALF])
        trig = sb("trig", [P, 2, 2, 2, HALF])
        bound = sb("bound", [P, 2, HALF])
        retr = sb("retr", [P, 2, FC, HALF])
        retr_sq = sb("retr_sq", [P, 2, FC, HALF])
        proj = sb("proj", [P, 2, TPH, D + 2])
        m_sq = sb("m_sq", [P, TPH])
        var2 = sb("var2", [P, TPH])
        var2e = sb("var2e", [P, 2, TPH])
        rstd2 = sb("rstd2", [P, 2, TPH])
        lg_sb = sb("lg_sb", [2 * E, 2, HALF])

        lg = x_sb[:, 0, 0:4, :].rearrange("p t d -> p (t d)")
        gate = x_sb[:, 0, 4:8, :].rearrange("p t d -> p (t d)")
        gate2 = x_sb[:, 1, 0:4, :].rearrange("p t d -> p (t d)")
        rank_key = x_sb[:, 1, 4:8, :].rearrange("p t d -> p (t d)")
        back_i = base_sb[:, 0, 0:4, :].rearrange("p t d -> p (t d)").bitcast(I32)
        back = base_sb[:, 0, 4:8, :].rearrange("p t d -> p (t d)")
        top8 = sb("top8", [P, 2, 8])
        picked = sb("picked", [P, K])
        row_base = sb("row_base", [P, EXPERT_UNITS], I32)
        row_ids = sb("row_ids", [P, EXPERT_UNITS], I32)

        trig_flat = trig[:, :, :, :, :].rearrange("p s c n t -> p (s c n t)")
        tanh_flat = tanhs[:, :, :, :].rearrange("p s n t -> p (s n t)")
        xg = trig_flat[:, 0:4 * GROW].rearrange("p (s w) -> p s w", s=4)
        xp = trig_flat[:, 4 * GROW:4 * GROW + 4 * D].rearrange("p (s w) -> p s w", s=4)
        xg_t = trig_flat[:, 3072:3584].rearrange("p (s c k) -> p s c k", s=2, c=2)
        qkv = retr_sq[:, :, :, :].rearrange("p s c t -> p (s c t)")[:, 0:4 * QW].rearrange("p (s w) -> p s w", s=4)
        qk_t = tanh_flat[:, 512:1024].rearrange("p (s n w) -> p s n w", s=2, n=2)
        probs = tanh_flat[:, 1024:1280].rearrange("p (s w) -> p s w", s=2)
        probs_t = tanh_flat[:, 1280:1536].rearrange("p (s w) -> p s w", s=2)
        av_t = tanh_flat[:, 1536:1792].rearrange("p (s w) -> p s w", s=2)
        ids_in = sb("ids_in", [P, 4], I32)
        ids_out = sb("ids_out", [P, 4], I32)
        turn_a = sb("turn_a", [P, 2, 2, 2, RH])
        turn_b = sb("turn_b", [P, 2, 2, 2, RH])
        neg_max = sb("neg_max", [P, 2])
        scratch_s = sb("scratch_s", [P, K])
        row_sum = sb("row_sum", [P, 4])
        gate_e = sb("gate_e", [P, 4])
        denom = sb("denom", [P, 1])
        row_scale = sb("row_scale", [P, 2])

        ps = [ctx.enter_context(nc.psum_tensor(f"bank{i}", [P, 512], F32)) for i in range(8)]

        w_in, vec_in, bo_in, wr_in, rope_in, ffn_in, wfo_in = [sem(n) for n in
            ("w_in", "vec_in", "bo_in", "wr_in", "rope_in", "ffn_in", "wfo_in")]
        pool_set, dve_set = sem("pool_set"), sem("dve_set")
        dve_passed, pool_passed = sem("dve_passed"), sem("pool_passed")
        wt_mm, wt_done, vec_mm, vec_done, fold_mm, fold_done, w_hi_done, split_done = [sem(n) for n in
            ("wt_mm", "wt_done", "vec_mm", "vec_done", "fold_mm", "fold_done",
             "w_hi_done", "split_done")]
        x_in = [[sem(f"x_in{slot}_{i}") for i in range(TPB // 2)] for slot in range(2)]
        xn_out = [sem("xn_out0"), sem("xn_out1")]
        lg_out = [sem("lg_out0"), sem("lg_out1")]
        out_out = [sem("out_out0"), sem("out_out1")]
        (bn_done, mv_done, ve_done, rstd_done, shift_done, xn_done, tp_mm, stage_done, hi_done, lo_done, lg_mm, lg_copied,
         k_mm, q_mm, v_mm,
         tanh_done, whole_done, frac_done, abs_done, trig_done, bound_done, memory_done, turned_done, retr_done,
         square_done, proj_mm, proj_done, msq_done, var_done, var2e_done, rstd2_done, final_done, base1_done,
         base_done) = [sem(n) for n in (
            "bn_done", "mv_done", "ve_done", "rstd_done", "shift_done", "xn_done", "tp_mm", "stage_done", "hi_done", "lo_done",
            "lg_mm", "lg_copied",
            "k_mm", "q_mm", "v_mm", "tanh_done", "whole_done", "frac_done", "abs_done", "trig_done", "bound_done",
            "memory_done", "turned_done", "retr_done", "square_done", "proj_mm", "proj_done", "msq_done",
            "var_done", "var2e_done", "rstd2_done", "final_done", "base1_done", "base_done")]
        lg_in, exp_done, gate_step, top_step, ids_mm, ids_done, row_base_set, wr_col_done = [sem(n) for n in (
            "lg_in", "exp_done", "gate_step", "top_step", "ids_mm", "ids_done", "row_base_set",
            "wr_col_done")]
        gathered = [sem(f"gathered{i}") for i in range(4)]
        scattered = [sem(f"scattered{i}") for i in range(4)]
        (ids_in_set, ids_out_set, xg_mm, xgt_done, qkv_mm, turn_done, rope_done, qkv_done,
         gate_done, qkt_mm, qkt_done, score_mm, max_done, prob_done, probt_mm, probt_done, av_mm,
         av_done, xp_mm, denom_done, scale_done, xp_done) = [sem(n) for n in (
            "ids_in_set", "ids_out_set", "xg_mm", "xgt_done", "qkv_mm", "turn_done", "rope_done",
            "qkv_done", "gate_done", "qkt_mm", "qkt_done", "score_mm", "max_done", "prob_done",
            "probt_mm", "probt_done", "av_mm", "av_done", "xp_mm", "denom_done", "scale_done", "xp_done")]

        block = ctx.enter_context(nc.Block())

        def wait(eng, s, count):
            if not isinstance(count, int) or count > 0:
                eng.wait_ge(s, count)

        def settle(eng, passed):
            eng.sem_inc(passed, 1)

        def run_steps(eng, step):
            for s in range(-4, 8):
                step(s // 8, s % 8, s)
            with eng.Fori(1, UNITS // 8 - 1) as k:
                for m in range(8):
                    step(k, m, None)
            for s in range(UNITS - 8, UNITS + 7):
                step(s // 8, s % 8, s)

        def has(s, lo, hi):
            return s is None or lo <= s < hi

        def run_expert_steps(eng, step):
            for i in range(-3, 4):
                step(i // 4, i % 4, i)
            with eng.Fori(1, EXPERT_UNITS // 4 - 1) as k:
                for m in range(4):
                    step(k, m, None)
            for i in range(EXPERT_UNITS - 4, EXPERT_UNITS + 3):
                step(i // 4, i % 4, i)

        x_tiles = x.rearrange("b (t p) d -> b p t d", p=P)
        out_tiles = out.rearrange("b (t p) d -> b p t d", p=P)
        out_rows = out.rearrange("b t d -> (b t) d")
        xn_tiles = xn_rows.rearrange("(b t p) d -> b p t d", b=NB, p=P)

        @block.sync
        def _(sp):
            def load_x(b, slot, i):
                sp.dma_start(x_sb[:, slot, 2 * i:2 * i + 2], x_tiles[b][:, 2 * i:2 * i + 2]
                             ).then_inc(x_in[slot][i], 16)

            for i in range(TPB // 2):
                load_x(0, 0, i)
            for n, w in enumerate((Wk, Wq, Wkp, Wqp, Wv, Wo)):
                sp.dma_start(w_nat[:, n], w.rearrange("(a p) d -> p a d", p=P)).then_inc(w_in, 16)
            for n, v in enumerate((bk, bq, bkp, bqp, bv, phase_scale, ln_g, ln_b)):
                sp.dma_start(vec_rows[2 * n:2 * n + 2, :], v.rearrange("(a p) -> a p", p=P)).then_inc(vec_in, 16)
            sp.dma_start(bo_row[:, :], bo.rearrange("(a n) -> a n", a=1)).then_inc(bo_in, 16)
            sp.dma_start(wr_nat[:, :], Wr).then_inc(wr_in, 16)
            for slot in range(2):
                sp.dma_start(xn_sb[:, slot, :, D:GROW], rope.rearrange("(t p) d -> p t d", p=P)
                             ).then_inc(rope_in, 16)
            for i in range(TPB // 2):
                load_x(1, 1, i)

            def step(k, m, s):
                b = 2 * k + m // 4
                slot = (m // 4) % 2
                if m % 4 == 1 and has(s, 0, UNITS):
                    sp.wait_ge(xn_done, 8 * b + 8)
                    if s is not None and s < 4:
                        sp.wait_ge(rope_in, 32)
                    sp.dma_start(xn_tiles[b], xn_sb[:, slot]).then_inc(xn_out[slot], 16)
                if m % 2 == 1 and has(s, 1, UNITS):
                    half = m // 2 % 2
                    sp.wait_ge(lg_copied, 4 * k + m // 2 + 1)
                    for part in range(2):
                        sp.dma_start(logit_rows[part, b][:, half * HALF:(half + 1) * HALF],
                                     lg_sb[part * E:(part + 1) * E, half, :]).then_inc(lg_out[half], 16)
                if has(s, 2, UNITS - 6):
                    xb = 2 * k + (m - 2) // 4
                    sp.wait_ge(base1_done, 8 * k + m - 1)
                    load_x(xb + 2, ((m - 2) // 4) % 2, (m - 2) % 4)
                if m % 2 == 0 and has(s, 8, UNITS + 7):
                    h_b, j = 2 * k + (m - 8) // 4, ((m - 8) // 2) % 2
                    sp.wait_ge(final_done, 4 * (4 * k + (m - 8) // 2) + 4)
                    sp.dma_start(out_tiles[h_b][:, TPH * j:TPH * j + TPH, :],
                                 base_sb[:, ((m - 8) // 4) % 2, TPH * j:TPH * j + TPH, :]).then_inc(out_out[j], 16)

            run_steps(sp, step)
            for half in range(2):
                sp.wait_ge(lg_out[half], 32 * NB)
            sp.wait_ge(base_done, UNITS)
            for part, place in enumerate((lg, gate)):
                sp.dma_start(place, logit_rows[part].rearrange("b e t -> (b e) t")).then_inc(lg_in, 16)
            sp.wait_ge(trig_done, 2 * UNITS)
            sp.dma_start(w_fo, Wfo.rearrange("e j d -> j e d")).then_inc(wfo_in, 16)
            for j in range(2):
                sp.wait_ge(xn_out[j], 16 * NB // 2)
            for e in range(E):
                sp.dma_start(w_qkv[:, e, :, 0:3 * HP], Wqkv[e].rearrange("(h p) j -> p h j", p=P)
                             ).then_inc(ffn_in, 16)
            for j in range(2):
                sp.wait_ge(out_out[j], 16 * NB)

        @block.tensor
        def _(pe):
            pe.wait_ge(pool_set, 4)
            pe.wait_ge(w_in, 16 * 6)
            for n in range(4):
                for a in range(2):
                    for c in range(2):
                        mm = pe.transpose(ps[n][:, c * D + a * P:c * D + (a + 1) * P],
                                          w_nat[:, 2 + n, a, c * P:(c + 1) * P], ident[:, :])
                mm.then_inc(wt_mm, 1)
            pe.wait_ge(vec_in, 16 * 8)
            pe.transpose(ps[4][:, 0:16], vec_rows[:, :], ident[0:16, 0:16]).then_inc(vec_mm, 1)
            pe.wait_ge(wr_in, 16)
            for c in range(2):
                mm = pe.transpose(ps[5][:, c * E:(c + 1) * E], wr_nat[:, c * P:(c + 1) * P], ident[0:E, 0:E])
            mm.then_inc(vec_mm, 1)
            pe.wait_ge(wt_done, 4)
            pe.wait_ge(vec_done, 2)
            for n in range(2):
                for c in range(2):
                    for a in range(2):
                        mm = pe.matmul(ps[n][:, c * D:(c + 1) * D], w_nat[:, n, a, c * P:(c + 1) * P],
                                       w_tr[:, n, a, :], start=(a == 0), stop=(a == 1))
                mm.then_inc(fold_mm, 1)
            for n in range(2):
                for c in range(2):
                    for a in range(2):
                        mm = pe.matmul(ps[2][:, 2 * n + c:2 * n + c + 1], w_tr[:, n, a, c * P:(c + 1) * P],
                                       vec[:, n, a:a + 1], start=(a == 0), stop=(a == 1))
            mm.then_inc(fold_mm, 1)
            pe.wait_ge(dve_set, 6)
            for c in range(2):
                mm = pe.matmul(ps[3][:, 0:D], mean_w[:, :], wo_g[:, c, :], start=(c == 0), stop=(c == 1))
            mm.then_inc(fold_mm, 1)
            pe.wait_ge(bo_in, 16)
            for c in range(2):
                pe.matmul(ps[6][:, 0:D], lnb_cols[:, c, :], w_tr[:, 3, c, :], start=(c == 0), stop=False)
            pe.matmul(ps[6][:, 0:D], ones[0:1, :], bo_row[:, :], start=False, stop=True).then_inc(fold_mm, 1)
            pe.wait_ge(fold_done, 3)
            pe.wait_ge(split_done, 6)

            K_BANK, Q_BANK, TP_BANK, LG_BANK = ps[0], ps[1], ps[4], ps[5]

            def step(k, m, s):
                u = 8 * k + m
                b = 2 * k + m // 4
                j, f = (m // 2) % 2, m % 2
                slot = (m // 4) % 2
                if has(s, 0, UNITS):
                    wait(pe, lo_done, u - m % 2 + 2)
                    for n, bank, ready in ((0, K_BANK, k_mm), (1, Q_BANK, q_mm), (2, ps[2 + m % 2], v_mm)):
                        if n < 2:
                            wait(pe, tanh_done, 2 * u - 1 + n)
                        else:
                            wait(pe, bound_done, u - 1)
                        for g, (wp, part) in enumerate(((0, xn_lo), (1, xn_hi), (0, xn_hi))):
                            for c in range(2):
                                mm = pe.matmul(bank[:, :], w_split[:, n, c, wp, f * P:(f + 1) * P],
                                               part[:, j, c, :], start=(g + c == 0), stop=(g + c == 3))
                        mm.then_inc(ready, 1)
                    if m % 2 == 0:
                        wait(pe, lg_copied, 4 * k + m // 2)
                    for c in range(2):
                        mm = pe.matmul(LG_BANK[0:2 * E, :], wr_split[:, c, :, :].rearrange("p h e -> p (h e)"),
                                       (xn_lo, xn_hi)[m % 2][:, j, c, :], start=(m % 2 + c == 0),
                                       stop=(m % 2 + c == 2))
                    if m % 2 == 1:
                        mm.then_inc(lg_mm, 1)
                if has(s, -3, PAIRS + 1):
                    q, mq = u - 1, (m - 1) % 8
                    wait(pe, xn_done, 2 * q + 10)
                    wait(pe, hi_done, q + 4)
                    for t in range(2):
                        for c in range(2):
                            mm = pe.transpose(TP_BANK[:, c * D + t * P:c * D + (t + 1) * P],
                                              xn_sb[:, (mq // 4 + 1) % 2, 2 * (mq % 4) + t, c * P:(c + 1) * P],
                                              ident[:, :])
                    mm.then_inc(tp_mm, 1)
                first = m % 2 == 0
                if has(s, 4, UNITS + 4):
                    h, mh = 4 * k + (m - (4 if first else 5)) // 2, ((m - (4 if first else 5)) // 2) % 2
                    wait(pe, square_done, 2 * h + 2)
                    for t in range(0, 2) if first else range(2, 4):
                        bank = ps[6 + t % 2]
                        wait(pe, proj_done, 4 * h + t - 1)
                        for c in range(2):
                            pe.matmul(bank[:, 0:D + 1], retr[:, mh, c, t * P:(t + 1) * P], wo_c[:, c, :],
                                      start=(c == 0), stop=(c == 1))
                        for c in range(2):
                            mm = pe.matmul(bank[:, D + 1:D + 2], retr_sq[:, mh, c, t * P:(t + 1) * P],
                                           ones[:, 0:1], start=(c == 0), stop=(c == 1))
                        mm.then_inc(proj_mm, 1)

            run_steps(pe, step)

            pe.wait_ge(top_step, 64)
            pe.wait_ge(proj_done, 4 * HALVES)
            pe.transpose(ps[0][:, 0:P], picked[:, :], ident[:, :]).then_inc(ids_mm, 1)
            pe.wait_ge(ids_done, 1)
            pe.wait_ge(wfo_in, 16)
            pe.wait_ge(ffn_in, 16 * E)
            pe.wait_ge(wr_col_done, 1)

            def expert_step(k, m, i):
                n = 4 * k + m
                if has(i, 0, EXPERT_UNITS):
                    wait(pe, xgt_done, n + 1)
                    for c in range(2):
                        mm = pe.matmul(ps[1][:, 0:QW], xg_t[:, m % 2, c, :], w_qkv[:, k // 4, c, :],
                                       start=(c == 0), stop=(c == 1))
                    mm.then_inc(qkv_mm, 1)
                if has(i, 1, EXPERT_UNITS + 1):
                    wait(pe, rope_done, n)
                    for t in range(2):
                        mm = pe.transpose(ps[2][:, t * K:(t + 1) * K], qkv[:, (m - 1) % 4, t * HP:(t + 1) * HP],
                                          ident[:, :])
                    mm.then_inc(qkt_mm, 1)
                if has(i, 2, EXPERT_UNITS + 2):
                    wait(pe, prob_done, n - 1)
                    pe.transpose(ps[4][:, 0:K], probs[:, m % 2, :], ident[:, :]).then_inc(probt_mm, 1)
                if has(i, -1, EXPERT_UNITS - 1):
                    g = (m + 1) % 4
                    pe.wait_ge(gathered[g], 16 * (k + (m + 1) // 4) + 16)
                    for c in range(2):
                        mm = pe.transpose(ps[0][:, c * P:(c + 1) * P], xg[:, g, c * P:(c + 1) * P], ident[:, :])
                    mm.then_inc(xg_mm, 1)
                if has(i, 3, EXPERT_UNITS + 3):
                    wait(pe, av_done, n - 2)
                    if i is not None and i > EXPERT_UNITS:
                        wait(pe, xp_done, n - 4)
                    pe.matmul(ps[6 + (m - 3) % 2][:, 0:D], av_t[:, (m - 3) % 2, :],
                              w_fo[:, (k + (m - 3) // 4) // 4, :], start=True, stop=True).then_inc(xp_mm, 1)
                if has(i, 1, EXPERT_UNITS + 1):
                    u = (m - 1) % 2
                    wait(pe, qkt_done, n)
                    pe.matmul(ps[3][:, 0:K], qk_t[:, u, 0, :], qk_t[:, u, 1, :], start=True, stop=False)
                    pe.matmul(ps[3][:, 0:K], ident_bf[:, :], causal[:, :], start=False, stop=True
                              ).then_inc(score_mm, 1)
                if has(i, 2, EXPERT_UNITS + 2):
                    wait(pe, probt_done, n - 1)
                    pe.matmul(ps[5][:, 0:K], qkv[:, (m - 2) % 4, 2 * HP:3 * HP], probs_t[:, m % 2, :],
                              start=True, stop=True).then_inc(av_mm, 1)

            run_expert_steps(pe, expert_step)

        @block.scalar
        def _(act):
            nc.scalar.preload_act_table_set("silu_and_others")
            for n in range(4):
                act.wait_ge(wt_mm, n + 1)
                nc.scalar.activation(w_tr[:, n], ps[n][:, :].rearrange("p (c d) -> p c d", c=2), ACT.Copy
                                     ).then_inc(wt_done, 1)
            act.wait_ge(vec_mm, 1)
            nc.scalar.activation(vec[:, :, :], ps[4][:, 0:16].rearrange("p (n a) -> p n a", a=2), ACT.Copy
                                 ).then_inc(vec_done, 1)
            act.wait_ge(vec_mm, 2)
            nc.scalar.activation(wr_t[:, :, :], ps[5][:, 0:2 * E].rearrange("p (c e) -> p c e", c=2), ACT.Copy
                                 ).then_inc(vec_done, 1)
            for n in range(2):
                act.wait_ge(fold_mm, n + 1)
                nc.scalar.activation(w_split[:, n, :, 0, :], ps[n][:, :].rearrange("p (c d) -> p c d", c=2),
                                     ACT.Copy).then_inc(w_hi_done, 1)

            def step(k, m, s):
                u = 8 * k + m
                b = 2 * k + m // 4
                f, slot = m % 2, (m // 4) % 2
                q, mq = u - 1, (m - 1) % 8
                if has(s, -3, PAIRS + 1):
                    qslot = (mq // 4 + 1) % 2
                    if mq % 4 == 0:
                        wait(act, xn_out[qslot], 16 * (k + ((m - 1) // 4 + 1) // 2))
                    wait(act, base1_done, u - 4)
                    wait(act, shift_done, q + 5)
                    for t in range(2):
                        nc.scalar.activation(xn_sb[:, qslot, 2 * (mq % 4) + t, 0:D],
                                             x_sb[:, qslot, 2 * (mq % 4) + t, :], ACT.Identity,
                                             bias=shift[:, mq % 2, t:t + 1], scale=rstd[:, mq % 2, t:t + 1]
                                             ).then_inc(xn_done, 1)
                if has(s, 0, UNITS):
                    wait(act, frac_done, u - 1)
                    for n, (bank, ready) in enumerate(((ps[0], k_mm), (ps[1], q_mm))):
                        act.wait_ge(ready, u + 1)
                        nc.scalar.activation(tanhs[:, m % 2, n, :], bank[:, :], ACT.Tanh,
                                             bias=kq_bias[:, n, f:f + 1]).then_inc(tanh_done, 1)
                if has(s, 1, UNITS + 1):
                    p = (m - 1) % 2
                    wait(act, frac_done, u)
                    wait(act, turned_done, u - 2)
                    nc.scalar.activation(frac_abs[:, p], frac[:, p], ACT.Abs).then_inc(abs_done, 1)
                    nc.scalar.activation(trig[:, p, 1], frac[:, p], ACT.Sin, scale=TWO_PI).then_inc(trig_done, 1)
                    wait(act, abs_done, u)
                    nc.scalar.activation(trig[:, p, 0], frac_abs[:, p], ACT.Sin, scale=-TWO_PI,
                                         bias=halfpi[:, 0:1]).then_inc(trig_done, 1)
                if has(s, 2, UNITS + 2):
                    wait(act, retr_done, u - 1)
                    wait(act, proj_mm, 4 * (4 * k + (m - 2) // 2) - 4)
                    r = ((m - 2) // 2) % 2
                    nc.scalar.activation(retr_sq[:, r, f, :], retr[:, r, f, :], ACT.Square
                                         ).then_inc(square_done, 1)
                first = m % 2 == 0
                if has(s, 4, UNITS + 4):
                    h, mh = 4 * k + (m - (4 if first else 5)) // 2, ((m - (4 if first else 5)) // 2) % 2
                    wait(act, final_done, 4 * h - (6 if first else 4))
                    for t in range(0, 2) if first else range(2, 4):
                        wait(act, proj_mm, 4 * h + t + 1)
                        nc.scalar.activation(proj[:, mh, t, :], ps[6 + t % 2][:, 0:D + 2], ACT.Copy
                                             ).then_inc(proj_done, 1)
                if m % 2 == 1 and has(s, 1, UNITS):
                    wait(act, lg_mm, 4 * k + m // 2 + 1)
                    wait(act, lg_out[m // 2 % 2], 32 * b)
                    nc.scalar.activation(lg_sb[:, m // 2 % 2, :], ps[5][0:2 * E, :], ACT.Copy
                                         ).then_inc(lg_copied, 1)
                if has(s, -3, PAIRS + 1):
                    wait(act, tp_mm, q + 5)
                    wait(act, lo_done, q + 3)
                    both = ps[4][:, :].rearrange("p (c d) -> p c d", c=2)
                    nc.scalar.activation(xn_stage[:, mq % 2], both, ACT.Copy).then_inc(stage_done, 1)
                    nc.scalar.activation(xn_hi[:, mq // 2 % 2, :, mq % 2 * D:(mq % 2 + 1) * D], both, ACT.Copy
                                         ).then_inc(hi_done, 1)

            run_steps(act, step)
            nc.scalar.preload_act_table_set("exp_and_others")
            act.wait_ge(gate_step, 1)
            nc.scalar.activation(gate, lg, ACT.Exp, scale=-1.0).then_inc(exp_done, 1)

            def expert_step(k, m, i):
                n = 4 * k + m
                if has(i, 0, EXPERT_UNITS):
                    wait(act, qkv_mm, n + 1)
                    nc.scalar.activation(qkv[:, m, :], ps[1][:, 0:QW], ACT.Copy).then_inc(qkv_done, 1)
                if has(i, 2, EXPERT_UNITS + 2):
                    wait(act, probt_mm, n - 1)
                    nc.scalar.activation(probs_t[:, m % 2, :], ps[4][:, 0:K], ACT.Copy).then_inc(probt_done, 1)
                if has(i, -1, EXPERT_UNITS - 1):
                    wait(act, xg_mm, n + 2)
                    nc.scalar.activation(xg_t[:, (m + 1) % 2], ps[0][:, 0:D].rearrange("p (c k) -> p c k", c=2),
                                         ACT.Copy).then_inc(xgt_done, 1)
                if has(i, 1, EXPERT_UNITS + 1):
                    mp = (m - 1) % 4
                    wait(act, max_done, n)
                    nc.scalar.activation(probs[:, mp % 2, :], ps[3][:, 0:K], ACT.Exp, scale=SCALE,
                                         bias=neg_max[:, mp % 2:mp % 2 + 1], accum_out=row_sum[:, mp:mp + 1]
                                         ).then_inc(prob_done, 1)
                    wait(act, qkv_done, n)
                    nc.scalar.activation(gate_e[:, mp:mp + 1], qkv[:, mp, 3 * HP:QW], ACT.Exp, scale=-1.0
                                         ).then_inc(gate_done, 1)
                if has(i, 2, EXPERT_UNITS + 2):
                    wait(act, av_mm, n - 1)
                    nc.scalar.activation(av_t[:, m % 2, :], ps[5][:, 0:K], ACT.Copy).then_inc(av_done, 1)

            act.wait_ge(ids_done, 1)
            run_expert_steps(act, expert_step)

        @block.vector
        def _(dve):
            nc.vector.memset(ones[:, :], 1.0).then_inc(dve_set, 1)
            nc.vector.memset(mean_w[:, :], 1.0 / D).then_inc(dve_set, 1)
            nc.vector.memset(halfpi[:, :], float(np.pi / 2))
            nc.vector.memset(power[:, :], -0.5)
            nc.vector.memset(restart[:, :], 1.0).then_inc(bn_done, 1)
            nc.vector.memset(wo_c[:, :, D:D + 1], 1.0)
            dve.wait_ge(bn_done, 1)
            nc.vector.memset(restart[:, :].rearrange("p (n c) -> p n c", c=CH)[:, :, 0:1], 0.0
                             ).then_inc(bn_done, 1)
            dve.wait_ge(vec_done, 1)
            dve.wait_ge(wt_done, 4)
            dve.wait_ge(dve_set, 2)
            for c in range(2):
                nc.vector.tensor_scalar(wo_g[:, c, :], w_tr[:, 3, c, :], vec[:, 6, c:c + 1], None, ALU.mult
                                        ).then_inc(dve_set, 1)
            nc.vector.tensor_scalar(turns[:, :], vec[:, 5, :], 1.0 / TWO_PI, None, ALU.mult)
            for c in range(2):
                nc.vector.tensor_scalar(lnb_cols[:, c, :], ones[:, :], vec[:, 7, c:c + 1], None, ALU.mult
                                        ).then_inc(dve_set, 1)
            def as_f32(ap):
                return ap.bitcast(F32)

            dve.wait_ge(vec_done, 2)
            nc.vector.tensor_copy(w_split[:, 2, :, 0, :], w_tr[:, 2]).then_inc(split_done, 1)
            nc.vector.tensor_copy(wr_split[:, :, 0, :], wr_t[:, :, :]).then_inc(split_done, 1)
            dve.wait_ge(split_done, 2)
            nc.vector.tensor_tensor(w_split[:, 2, :, 1, :], w_tr[:, 2], as_f32(w_split[:, 2, :, 0, :]), ALU.subtract
                                    ).then_inc(split_done, 1)
            nc.vector.tensor_tensor(wr_split[:, :, 1, :], wr_t[:, :, :], as_f32(wr_split[:, :, 0, :]), ALU.subtract
                                    ).then_inc(split_done, 1)
            for n in range(2):
                dve.wait_ge(w_hi_done, n + 1)
                nc.vector.tensor_tensor(w_split[:, n, :, 1, :], ps[n][:, :].rearrange("p (c d) -> p c d", c=2),
                                        as_f32(w_split[:, n, :, 0, :]), ALU.subtract).then_inc(split_done, 1)
            dve.wait_ge(fold_mm, 3)
            nc.vector.tensor_tensor(kq_bias[:, :, :], ps[2][:, 0:4].rearrange("p (n c) -> p n c", n=2),
                                    vec[:, 2:4, :], ALU.add).then_inc(fold_done, 1)
            dve.wait_ge(fold_mm, 4)
            nc.vector.tensor_tensor(wo_c[:, :, 0:D], wo_g[:, :, :],
                                    ps[3][:, 0:D].unsqueeze(1).to_broadcast([P, 2, D]), ALU.subtract
                                    ).then_inc(fold_done, 1)
            dve.wait_ge(fold_mm, 5)
            nc.vector.tensor_copy(const_row[:, :], ps[6][:, 0:D]).then_inc(fold_done, 1)
            dve.wait_ge(fold_done, 3)

            BN0 = 2

            def step(k, m, s):
                u = 8 * k + m
                f = m % 2
                has_pair, has_unit, had_unit = has(s, -4, PAIRS), has(s, 0, UNITS), has(s, 1, UNITS + 1)
                has_stats = m % 2 == 0 and has(s, 6, UNITS + 5)
                first = m % 2 == 1
                has_final = has(s, 7, UNITS + 7)
                slot = (m // 4 + 1) % 2
                p = (m - 1) % 2
                both = tanhs[:, m % 2].rearrange("p n t -> p (n t)")

                def final(t):
                    mf = m - (7 if first else 8)
                    mh = (mf // 2) % 2
                    row = base_sb[:, (mf // 4) % 2, TPH * mh + t, :]
                    nc.vector.scalar_tensor_tensor(out=row, in0=proj[:, mh, t, 0:D],
                                                   scalar=rstd2[:, mh, t:t + 1], in1=row,
                                                   op0=ALU.mult, op1=ALU.add).then_inc(final_done, 1)

                if has_pair:
                    wait(dve, x_in[slot][m % 4], 16 * (k + (m // 4 + 1) // 2) + 16)
                    for t in range(2):
                        nc.vector.bn_stats(bn[:, m % 2, t, :], x_sb[:, slot, 2 * (m % 4) + t, :]).then_inc(bn_done, 1)
                if has_unit:
                    if s == 1:
                        wait(dve, frac_done, 1)
                    wait(dve, tanh_done, 2 * u + 2)
                    nc.vector.tensor_scalar(whole[:, :], both, turns[:, f:f + 1], ROUND, ALU.mult, ALU.add
                                            ).then_inc(whole_done, 1)
                if has_pair:
                    wait(dve, shift_done, u + 3)
                    dve.wait_ge(bn_done, BN0 + 2 * u + 10)
                    settle(dve, dve_passed)
                    for t in range(2):
                        nc.vector.bn_aggr(mv[:, m % 2, t, :], bn[:, m % 2, t, :]).then_inc(mv_done, 1)
                if has_unit:
                    wait(dve, trig_done, 2 * u - 2)
                    dve.wait_ge(whole_done, u + 1)
                    nc.vector.scalar_tensor_tensor(
                        out=frac[:, m % 2].rearrange("p n t -> p (n t)"), in0=both, scalar=turns[:, f:f + 1],
                        in1=whole[:, :].bitcast(I16).rearrange("p (t w) -> p t w", w=2)[:, :, 0],
                        op0=ALU.mult, op1=ALU.subtract).then_inc(frac_done, 1)
                if has_final:
                    if first:
                        wait(dve, base_done, 8 * k + m - 5)
                        wait(dve, rstd2_done, 4 * k + (m - 7) // 2 + 1)
                    final(0 if first else 2)
                if has_stats:
                    h, mh = 4 * k + (m - 6) // 2, ((m - 6) // 2) % 2
                    total, total_sq = proj[:, mh, :, D], proj[:, mh, :, D + 1]
                    wait(dve, proj_done, 4 * h + 4)
                    nc.vector.scalar_tensor_tensor(out=m_sq[:, :], in0=total, scalar=1.0 / (D * D), in1=total,
                                                   op0=ALU.mult, op1=ALU.mult).then_inc(msq_done, 1)
                if had_unit:
                    wait(dve, v_mm, u)
                    wait(dve, trig_done, 2 * u)
                    nc.vector.scalar_tensor_tensor(
                        out=bound[:, :, :], in0=ps[2 + p][:, :].unsqueeze(1).to_broadcast([P, 2, HALF]),
                        scalar=vec[:, 4, p:p + 1], in1=trig[:, p, :, 0, :], op0=ALU.add, op1=ALU.mult
                    ).then_inc(bound_done, 1)
                if has_stats:
                    wait(dve, msq_done, h + 1)
                    nc.vector.scalar_tensor_tensor(out=var2[:, :], in0=total_sq, scalar=1.0 / D, in1=m_sq[:, :],
                                                   op0=ALU.mult, op1=ALU.subtract).then_inc(var_done, 1)
                if had_unit:
                    wait(dve, bound_done, u)
                    nc.vector.tensor_tensor_scan(memory[:, :, :].rearrange("p n t -> p (n t)"), restart[:, :],
                                                 bound[:, :, :].rearrange("p n t -> p (n t)"), 0.0,
                                                 ALU.mult, ALU.add).then_inc(memory_done, 1)
                if has_stats:
                    wait(dve, rstd2_done, h - 1)
                    wait(dve, var_done, h + 1)
                    nc.vector.tensor_scalar(var2e[:, mh, :], var2[:, :], 0.0, EPS * D, ALU.max, ALU.add
                                            ).then_inc(var2e_done, 1)
                if has_final:
                    final(1 if first else 3)
                if had_unit:
                    wait(dve, retr_done, u - 2)
                    wait(dve, memory_done, u)
                    nc.vector.tensor_tensor(turned[p][:, :, :], memory[:, :, :], trig[:, p, :, 1, :], ALU.mult
                                            ).then_inc(turned_done, 1)

            run_steps(dve, step)

            dve.wait_ge(lg_in, 32)
            nc.vector.tensor_tensor(lg, lg, gate, ALU.add).then_inc(gate_step, 1)
            dve.wait_ge(exp_done, 1)
            nc.vector.tensor_scalar(gate, gate, 1.0, None, ALU.add).then_inc(gate_step, 1)
            dve.wait_ge(gate_step, 2)
            nc.vector.reciprocal(gate2, gate).then_inc(gate_step, 1)
            dve.wait_ge(gate_step, 3)
            steps = 0

            def top_rounds(values, replaced_by, keep):
                nonlocal steps
                for r in range(K // 8):
                    eight = picked[:, 8 * r:8 * r + 8] if keep else top8[:, r % 2, :]
                    nc.vector.max(eight, values).then_inc(top_step, 1)
                    steps += 1
                    dve.wait_ge(top_step, steps)
                    nc.vector.match_replace(values, eight, values, replaced_by).then_inc(top_step, 1)
                    steps += 1
                    dve.wait_ge(top_step, steps)

            top_rounds(gate2, -1.0, False)
            dve.wait_ge(row_base_set, 2)
            nc.vector.tensor_copy(back, back_i).then_inc(gate_step, 1)
            dve.wait_ge(gate_step, 4)
            nc.vector.scalar_tensor_tensor(out=rank_key, in0=gate2, scalar=0.0, in1=back, op0=ALU.is_lt,
                                           op1=ALU.mult).then_inc(gate_step, 1)
            dve.wait_ge(gate_step, 5)
            top_rounds(rank_key, 0.0, True)
            for j in range(2):
                dve.wait_ge(xn_out[j], 16 * NB // 2)
            nc.vector.tensor_copy(w_qkv[:, :, :, 3 * HP:QW].rearrange("p e c o -> p e (c o)"),
                                  wr_t[:, :, :].rearrange("p c e -> p e c")).then_inc(wr_col_done, 1)
            dve.wait_ge(ids_mm, 1)
            by_expert = "p (e b) -> p e b"
            nc.vector.tensor_tensor(row_ids[:, :].rearrange(by_expert, e=E),
                                    row_base[:, :].rearrange(by_expert, e=E),
                                    ps[0][:, 0:P].rearrange("p (b e) -> p e b", e=E), ALU.subtract
                                    ).then_inc(ids_done, 1)

            def expert_step(k, m, i):
                n = 4 * k + m
                if has(i, 1, EXPERT_UNITS + 1):
                    wait(dve, qkt_mm, n)
                    nc.vector.tensor_copy(qk_t[:, (m - 1) % 2], ps[2][:, 0:2 * K].rearrange("p (t k) -> p t k", t=2)
                                          ).then_inc(qkt_done, 1)
                if has(i, 0, EXPERT_UNITS):
                    heads = qkv[:, m, 0:2 * HP]
                    rotated = heads.rearrange("p (t h r) -> p t h r", t=2, r=RH)[:, :, 0:2, :]
                    row = xg[:, m, :]
                    cos = row[:, D:D + RH].unsqueeze(1).unsqueeze(1).to_broadcast([P, 2, 2, RH])
                    wait(dve, qkv_done, n + 1)
                    nc.vector.tensor_tensor(turn_a[:, m % 2], rotated, cos, ALU.mult).then_inc(turn_done, 1)
                    for h in range(2):
                        sin = row[:, D + (1 + h) * RH:D + (2 + h) * RH].unsqueeze(1).to_broadcast([P, 2, RH])
                        nc.vector.tensor_tensor(turn_b[:, m % 2, :, h, :], rotated[:, :, 1 - h, :], sin, ALU.mult
                                                ).then_inc(turn_done, 1)
                    dve.wait_ge(turn_done, 3 * n + 3)
                    nc.vector.tensor_tensor(
                        heads.rearrange("p (t j) -> p t j", t=2)[:, :, 0:ROT], turn_a[:, m % 2].rearrange("p t h r -> p t (h r)"),
                        turn_b[:, m % 2].rearrange("p t h r -> p t (h r)"), ALU.add).then_inc(rope_done, 1)
                if has(i, 1, EXPERT_UNITS + 1):
                    u = (m - 1) % 2
                    wait(dve, score_mm, n)
                    nc.vector.tensor_scalar(scratch_s[:, :], ps[3][:, 0:K], -SCALE, None, ALU.mult, ALU.min,
                                            accum_out=neg_max[:, u:u + 1]).then_inc(max_done, 1)
                if has(i, 3, EXPERT_UNITS + 3):
                    u = (m - 3) % 4
                    wait(dve, gate_done, n - 2)
                    nc.vector.scalar_tensor_tensor(out=denom[:, :], in0=gate_e[:, u:u + 1], scalar=1.0,
                                                   in1=row_sum[:, u:u + 1], op0=ALU.add, op1=ALU.mult
                                                   ).then_inc(denom_done, 1)
                    wait(dve, denom_done, n - 2)
                    nc.vector.reciprocal(row_scale[:, u % 2:u % 2 + 1], denom[:, :]).then_inc(scale_done, 1)
                    wait(dve, scattered[u], 16 * (k + (m - 3) // 4))
                    wait(dve, xp_mm, n - 2)
                    wait(dve, scale_done, n - 2)
                    nc.vector.tensor_scalar(xp[:, u, :], ps[6 + u % 2][:, 0:D], row_scale[:, u % 2:u % 2 + 1], None,
                                            ALU.mult).then_inc(xp_done, 1)

            run_expert_steps(dve, expert_step)

        @block.gpsimd
        def _(pool):
            nc.gpsimd.memset(ident[:, :], 0.0).then_inc(pool_set, 1)
            nc.gpsimd.memset(causal[:, :], 0.0).then_inc(pool_set, 1)
            pool.wait_ge(pool_set, 2)
            nc.gpsimd.affine_select(out=ident[:, :], in_=ident[:, :], compare_op=ALU.not_equal, fill=1.0, base=0,
                                    pattern=[[-1, P]], channel_multiplier=1).then_inc(pool_set, 1)
            nc.gpsimd.affine_select(out=causal[:, :], in_=causal[:, :], compare_op=ALU.is_ge, fill=MASKED, base=0,
                                    pattern=[[-1, K]], channel_multiplier=1).then_inc(pool_set, 1)
            pool.wait_ge(pool_set, 4)
            nc.gpsimd.tensor_copy(ident_bf[:, :], ident[:, :]).then_inc(pool_set, 1)
            nc.gpsimd.iota(row_base[:, :], pattern=[[0, E], [SEQ, NB]], base=SEQ, channel_multiplier=0
                           ).then_inc(row_base_set, 1)
            pool.wait_ge(bn_done, 2)
            pool.wait_ge(fold_done, 3)

            def step(k, m, s):
                u = 8 * k + m
                if has(s, -2, PAIRS + 2):
                    mq = (m - 2) % 8
                    wait(pool, hi_done, u + 3)
                    place = (slice(None), mq // 2 % 2, slice(None), slice(mq % 2 * D, (mq % 2 + 1) * D))
                    nc.gpsimd.tensor_tensor(xn_lo[place], xn_stage[:, mq % 2], xn_hi[place].bitcast(F32),
                                            ALU.subtract).then_inc(lo_done, 1)
                if has(s, -4, PAIRS):
                    wait(pool, mv_done, 2 * u + 10)
                    wait(pool, xn_done, 2 * u + 6)
                    settle(pool, pool_passed)
                    nc.gpsimd.tensor_scalar(ve[:, m % 2, :], mv[:, m % 2, :, 1], EPS, None, ALU.add).then_inc(ve_done, 1)
                    nc.gpsimd.tensor_scalar(neg_mean[:, m % 2, :], mv[:, m % 2, :, 0], -1.0, None, ALU.mult
                                            ).then_inc(ve_done, 1)
                    pool.wait_ge(ve_done, 2 * u + 10)
                    nc.gpsimd.tensor_tensor(rstd[:, m % 2, :], ve[:, m % 2, :], power[:, 0:2], ALU.pow
                                            ).then_inc(rstd_done, 1)
                    pool.wait_ge(rstd_done, u + 5)
                    nc.gpsimd.tensor_tensor(shift[:, m % 2, :], neg_mean[:, m % 2, :], rstd[:, m % 2, :], ALU.mult
                                            ).then_inc(shift_done, 1)
                if has(s, 2, UNITS + 2):
                    b, slot, i = 2 * k + (m - 2) // 4, ((m - 2) // 4) % 2, (m - 2) % 4
                    if i == 0:
                        wait(pool, xn_done, 8 * b + 8)
                    if i % 2 == 0:
                        wait(pool, out_out[i // 2], 16 * (b - 1))
                    tiles = base_sb[:, slot, 2 * i:2 * i + 2]
                    nc.gpsimd.tensor_tensor(tiles, x_sb[:, slot, 2 * i:2 * i + 2],
                                            xn_sb[:, slot, 2 * i:2 * i + 2, 0:D], ALU.add).then_inc(base1_done, 1)
                    wait(pool, base1_done, u - 1)
                    nc.gpsimd.tensor_tensor(tiles, tiles, const_row[:, :].unsqueeze(1).to_broadcast([P, 2, D]),
                                            ALU.add).then_inc(base_done, 1)
                if has(s, 1, UNITS + 1):
                    wait(pool, turned_done, u)
                    wait(pool, proj_mm, 4 * (4 * k + (m - 1) // 2) - 4)
                    nc.gpsimd.tensor_tensor(retr[:, (m - 1) // 2 % 2, (m - 1) % 2, :], turned[(m - 1) % 2][:, 0, :],
                                            turned[(m - 1) % 2][:, 1, :], ALU.add).then_inc(retr_done, 1)
                if m % 2 == 0 and has(s, 6, UNITS + 5):
                    h, mh = 4 * k + (m - 6) // 2, ((m - 6) // 2) % 2
                    wait(pool, var2e_done, h + 1)
                    wait(pool, final_done, 4 * h - 4)
                    nc.gpsimd.tensor_tensor(rstd2[:, mh, :], var2e[:, mh, :], power[:, 0:TPH], ALU.pow
                                            ).then_inc(rstd2_done, 1)

            run_steps(pool, step)
            for j in range(2):
                pool.wait_ge(out_out[j], 16 * NB)
                pool.wait_ge(xn_out[j], 16 * NB // 2)
            nc.gpsimd.iota(back_i, pattern=[[-1, SEQ]], base=SEQ, channel_multiplier=0).then_inc(row_base_set, 1)
            pool.wait_ge(ids_done, 1)

            def expert_step(k, m, i):
                n = 4 * k + m
                if has(i, -3, EXPERT_UNITS - 3):
                    g = (m + 3) % 4
                    kg = k + (m + 3) // 4
                    wait(pool, gathered[g], 16 * kg)
                    wait(pool, rope_done, n)
                    wait(pool, xg_mm, n)
                    nc.gpsimd.tensor_copy(ids_in[:, g:g + 1], row_ids[:, bass.ds(n + 3, 1)]
                                          ).then_inc(ids_in_set, 1)
                    pool.wait_ge(ids_in_set, n + 4)
                    settle(pool, pool_passed)
                    nc.gpsimd.indirect_dma_start(
                        out=xg[:, g, :], out_offset=None, in_=xn_rows,
                        in_offset=bass.IndirectOffsetOnAxis(ap=ids_in[:, g:g + 1].bitcast(U32), axis=0)
                    ).then_inc(gathered[g], 16)
                if has(i, 3, EXPERT_UNITS + 3):
                    g = (m - 3) % 4
                    ks = k + (m - 3) // 4
                    wait(pool, scattered[g], 16 * ks)
                    nc.gpsimd.tensor_copy(ids_out[:, g:g + 1], row_ids[:, bass.ds(n - 3, 1)]
                                          ).then_inc(ids_out_set, 1)
                    pool.wait_ge(ids_out_set, n - 2)
                    wait(pool, xp_done, n - 2)
                    settle(pool, pool_passed)
                    nc.gpsimd.indirect_dma_start(
                        out=out_rows, out_offset=bass.IndirectOffsetOnAxis(ap=ids_out[:, g:g + 1].bitcast(U32),
                                                                           axis=0),
                        in_=xp[:, g, :], in_offset=None, compute_op=ALU.add).then_inc(scattered[g], 16)

            run_expert_steps(pool, expert_step)
            for g in range(4):
                pool.wait_ge(scattered[g], 16 * EXPERT_UNITS // 4)


def rope_rows():
    inv_freq = (1.0 / np.float32(10000.0) ** (np.arange(RH, dtype=np.float32) * np.float32(2.0) / np.float32(ROT))
                ).astype(np.float32)
    angle = np.arange(SEQ, dtype=np.float32)[:, None] * inv_freq
    cos, sin = np.cos(angle), np.sin(angle)
    return np.ascontiguousarray(np.concatenate([cos, -sin, sin], axis=1).astype(np.float32))


_INS = ["L0_attn_x", "L0_attn_Wk", "L0_attn_bk", "L0_attn_Wv", "L0_attn_bv", "L0_attn_Wq", "L0_attn_bq",
        "L0_attn_Wkp", "L0_attn_bkp", "L0_attn_Wqp", "L0_attn_bqp", "L0_attn_phase_scale", "L0_attn_ln_g",
        "L0_attn_ln_b", "L0_attn_Wo", "L0_attn_bo", "L0_ffn_Wr", "L0_ffn_Wqkv", "L0_ffn_Wo"]


def kernel(**inputs):
    import concourse.bacc as bacc
    from concourse.bass_utils import run_bass_kernel_spmd

    nc = bacc.Bacc("TRN2", target_bir_lowering=False, num_devices=1)
    arrays, args = {}, []
    for name in _INS:
        a = np.ascontiguousarray(inputs[name])
        arrays[f"in_{name}"] = a
        args.append(nc.dram_tensor(f"in_{name}", a.shape, mybir.dt.from_np(a.dtype), kind="ExternalInput").ap())
    arrays["rope_rows"] = rope_rows()
    args.append(nc.dram_tensor("rope_rows", [SEQ, 3 * RH], F32, kind="ExternalInput").ap())
    args.append(nc.dram_tensor("out_x", [NB, SEQ, D], F32, kind="ExternalOutput").ap())
    build(nc, *args)
    r = run_bass_kernel_spmd(nc, [arrays], core_ids=[0])
    return r.results[0]["out_x"]
```

```python
from contextlib import ExitStack

import numpy as np

import concourse.bass as bass
import concourse.mybir as mybir

F32 = mybir.dt.float32
F32R = mybir.dt.float32r
BF16 = mybir.dt.bfloat16
I32 = mybir.dt.int32
I16 = mybir.dt.int16
U32 = mybir.dt.uint32
ALU = mybir.AluOpType
ACT = mybir.ActivationFunctionType
AX = mybir.AxisListType

P = 128
NB, SEQ, D = 16, 1024, 256
NTOK = NB * SEQ
CH = 64
FC = D // P
HALF = 512
TPH = HALF // P
TPB = SEQ // P
UNITS = NB * (SEQ // HALF) * FC
PAIRS = UNITS - 4
HALVES = UNITS // 2
E, HP, ROT = 8, 128, 64
RH = ROT // 2
K = SEQ // 8
GROW = D + 3 * RH
QW = 3 * HP + 2
EPS = 1e-5
TWO_PI = float(2 * np.pi)
ROUND = float(1.5 * 2 ** 23)
MASKED = -1e30
SCALE = float(HP) ** -0.5
EXPERT_UNITS = NB * E


def build(nc, x, Wk, bk, Wv, bv, Wq, bq, Wkp, bkp, Wqp, bqp, phase_scale, ln_g, ln_b, Wo, bo, Wr, Wqkv, Wfo,
          rope, out):
    with ExitStack() as ctx:
        def sb(name, shape, dt=F32):
            return ctx.enter_context(nc.sbuf_tensor(name, shape, dt))

        def sem(name):
            return ctx.enter_context(nc.semaphore(name))

        xn_rows = nc.dram_tensor("xn_rows", [NTOK, GROW], F32, kind="Internal").ap()
        logit_rows = nc.dram_tensor("logit_rows", [2, NB, E, SEQ], F32, kind="Internal").ap()

        ident = sb("ident", [P, P])
        ident_bf = sb("ident_bf", [P, P], BF16)
        causal = sb("causal", [P, K], BF16)
        ones = sb("ones", [P, P])
        mean_w = sb("mean_w", [P, P])
        power = sb("power", [P, 8])
        halfpi = sb("halfpi", [P, 1])
        restart = sb("restart", [P, 2 * HALF])
        w_nat = sb("w_nat", [P, 6, 2, D])
        w_flat = w_nat[:, :, :, :].rearrange("p n a d -> p (n a d)")
        whole = w_flat[:, 0:2 * HALF]
        memory = w_flat[:, 2 * HALF:4 * HALF].rearrange("p (n t) -> p n t", n=2)
        turned = [w_flat[:, 4 * HALF:6 * HALF].rearrange("p (n t) -> p n t", n=2), sb("turned", [P, 2, HALF])]
        w_tr = sb("w_tr", [P, 4, 2, D])
        xn_stage = w_tr[:, 0:2]
        w_split = sb("w_split", [P, 3, 2, 2, D], F32R)
        wr_split = sb("wr_split", [P, 2, 2, E], F32R)
        wo_g = sb("wo_g", [P, 2, D])
        wo_c = sb("wo_c", [P, 2, D + 1])
        vec_rows = sb("vec_rows", [16, P])
        vec = sb("vec", [P, 8, 2])
        bo_row = sb("bo_row", [1, D])
        wr_nat = sb("wr_nat", [E, D])
        wr_t = sb("wr_t", [P, 2, E])
        kq_bias = sb("kq_bias", [P, 2, 2])
        turns = sb("turns", [P, 2])
        lnb_cols = sb("lnb_cols", [P, 2, P])
        const_row = sb("const_row", [P, D])

        x_sb = sb("x_sb", [P, 2, TPB, D])
        row_area = sb("row_area", [P, max(2 * TPB * GROW, E * 2 * QW)])
        xn_sb = row_area[:, 0:2 * TPB * GROW].rearrange("p (s t w) -> p s t w", s=2, t=TPB)
        w_qkv = row_area[:, 0:E * 2 * QW].rearrange("p (e h j) -> p e h j", e=E, h=2)
        w_rows = row_area[:, 0:E * 2 * QW].rearrange("p (r j) -> p r j", r=E * 2)
        base_sb = sb("base_sb", [P, 2, TPB, D])
        xn_split = sb("xn_split", [P, 2 * 2 * FC * HALF], F32R)
        xn_hi, xn_lo = [xn_split[:, n * 2 * FC * HALF:(n + 1) * 2 * FC * HALF].rearrange(
            "p (s c t) -> p s c t", s=2, c=FC) for n in range(2)]
        w_cur = xn_split[:, 0:4 * 2 * QW].rearrange("p (r h j) -> p r h j", r=4, h=2)
        bn = sb("bn", [P, 2, 2, 6])
        mv = sb("mv", [P, 2, 2, 2])
        ve = sb("ve", [P, 2, 2])
        neg_mean = sb("neg_mean", [P, 2, 2])
        shift = sb("shift", [P, 2, 2])
        rstd = sb("rstd", [P, 2, 2])
        tanhs = sb("tanhs", [P, 2, 2, HALF])
        frac = sb("frac", [P, 2, 2, HALF])
        frac_abs = sb("frac_abs", [P, 2, 2, HALF])
        trig = sb("trig", [P, 2, 2, 2, HALF])
        bound = sb("bound", [P, 2, HALF])
        retr = sb("retr", [P, 2, FC, HALF])
        retr_sq = sb("retr_sq", [P, 2, FC, HALF])
        proj = sb("proj", [P, 2, TPH, D + 2])
        m_sq = sb("m_sq", [P, TPH])
        var2 = sb("var2", [P, TPH])
        var2e = sb("var2e", [P, 2, TPH])
        rstd2 = sb("rstd2", [P, 2, TPH])
        lg_sb = sb("lg_sb", [2 * E, 2, HALF])

        lg = frac[:, 0].rearrange("p n t -> p (n t)")
        gate = frac[:, 1].rearrange("p n t -> p (n t)")
        gate2 = x_sb[:, 1, 0:4, :].rearrange("p t d -> p (t d)")
        rank_key = x_sb[:, 1, 4:8, :].rearrange("p t d -> p (t d)")
        back_i = base_sb[:, 0, 0:4, :].rearrange("p t d -> p (t d)").bitcast(I32)
        back = base_sb[:, 0, 4:8, :].rearrange("p t d -> p (t d)")
        top8 = sb("top8", [P, 2, 8])
        picked = sb("picked", [P, K])
        row_base = sb("row_base", [P, EXPERT_UNITS], I32)
        row_ids = sb("row_ids", [P, EXPERT_UNITS], I32)

        w_fo = x_sb[:, 0].rearrange("p t d -> p (t d)").rearrange("p (e d) -> p e d", e=E)
        trig_flat = trig[:, :, :, :, :].rearrange("p s c n t -> p (s c n t)")
        tanh_flat = tanhs[:, :, :, :].rearrange("p s n t -> p (s n t)")
        xg = trig_flat[:, 0:8 * GROW].rearrange("p (s w) -> p s w", s=8)
        xp = trig_flat[:, 8 * GROW:8 * GROW + 4 * D].rearrange("p (s w) -> p s w", s=4)
        xg_split = w_split[:, 0, :, :, :].rearrange("p c h d -> p (c h d)").rearrange(
            "p (s h w) -> p s h w", s=2, h=2)
        qkv = retr_sq[:, :, :, :].rearrange("p s c t -> p (s c t)")[:, 0:4 * QW].rearrange("p (s w) -> p s w", s=4)
        qk_t = tanh_flat[:, 512:1024].rearrange("p (s n w) -> p s n w", s=2, n=2)
        probs = tanh_flat[:, 1024:1280].rearrange("p (s w) -> p s w", s=2)
        probs_t = tanh_flat[:, 1280:1536].rearrange("p (s w) -> p s w", s=2)
        av_t = tanh_flat[:, 1536:1792].rearrange("p (s w) -> p s w", s=2)
        ids_in = sb("ids_in", [P, 8], I32)
        ids_out = sb("ids_out", [P, 8], I32)
        turn_a = sb("turn_a", [P, 2, 2, 2, RH])
        turn_b = sb("turn_b", [P, 2, 2, 2, RH])
        neg_max = sb("neg_max", [P, 2])
        scratch_s = sb("scratch_s", [P, K])
        row_sum = sb("row_sum", [P, 4])
        gate_e = sb("gate_e", [P, 4])
        denom = sb("denom", [P, 1])
        row_scale = sb("row_scale", [P, 2])

        ps = [ctx.enter_context(nc.psum_tensor(f"bank{i}", [P, 512], F32)) for i in range(8)]

        w_in, vec_in, bo_in, wr_in, rope_in, ffn_in, wfo_in = [sem(n) for n in
            ("w_in", "vec_in", "bo_in", "wr_in", "rope_in", "ffn_in", "wfo_in")]
        pool_set, dve_set = sem("pool_set"), sem("dve_set")
        dve_passed, pool_passed = sem("dve_passed"), sem("pool_passed")
        wt_mm, wt_done, vec_mm, vec_done, fold_mm, fold_done, w_hi_done, split_done = [sem(n) for n in
            ("wt_mm", "wt_done", "vec_mm", "vec_done", "fold_mm", "fold_done",
             "w_hi_done", "split_done")]
        x_in = [[sem(f"x_in{slot}_{i}") for i in range(TPB // 2)] for slot in range(2)]
        xn_out = [sem("xn_out0"), sem("xn_out1")]
        lg_out = [sem("lg_out0"), sem("lg_out1")]
        out_out = [sem("out_out0"), sem("out_out1")]
        (bn_done, mv_done, ve_done, rstd_done, shift_done, xn_done, tp_mm, stage_done, hi_done, lo_done,
         lg_mm, lg_copied,
         k_mm, q_mm, v_mm,
         tanh_done, whole_done, frac_done, abs_done, trig_done, bound_done, memory_done, turned_done, retr_done,
         square_done, proj_mm, proj_done, msq_done, var_done, var2e_done, rstd2_done, final_done, base1_done,
         base_done) = [sem(n) for n in (
            "bn_done", "mv_done", "ve_done", "rstd_done", "shift_done", "xn_done", "tp_mm", "stage_done", "hi_done",
            "lo_done",
            "lg_mm", "lg_copied",
            "k_mm", "q_mm", "v_mm", "tanh_done", "whole_done", "frac_done", "abs_done", "trig_done", "bound_done",
            "memory_done", "turned_done", "retr_done", "square_done", "proj_mm", "proj_done", "msq_done",
            "var_done", "var2e_done", "rstd2_done", "final_done", "base1_done", "base_done")]
        lg_in, exp_done, gate_step, top_step, ids_mm, ids_done, row_base_set, wr_col_done = [sem(n) for n in (
            "lg_in", "exp_done", "gate_step", "top_step", "ids_mm", "ids_done", "row_base_set",
            "wr_col_done")]
        gathered = [sem(f"gathered{i}") for i in range(8)]
        scattered = [sem(f"scattered{i}") for i in range(4)]
        (ids_in_set, ids_out_set, xg_mm, xg_hi_done, xg_lo_done, wx_hi_done, wx_lo_done, qkv_mm,
         turn_done, rope_done, qkv_done,
         gate_done, qkt_mm, qkt_done, score_mm, max_done, prob_done, probt_mm, probt_done, av_mm,
         av_done, xp_mm, denom_done, scale_done, xp_done) = [sem(n) for n in (
            "ids_in_set", "ids_out_set", "xg_mm", "xg_hi_done", "xg_lo_done", "wx_hi_done", "wx_lo_done",
            "qkv_mm", "turn_done", "rope_done",
            "qkv_done", "gate_done", "qkt_mm", "qkt_done", "score_mm", "max_done", "prob_done",
            "probt_mm", "probt_done", "av_mm", "av_done", "xp_mm", "denom_done", "scale_done", "xp_done")]

        block = ctx.enter_context(nc.Block())

        def wait(eng, s, count):
            if not isinstance(count, int) or count > 0:
                eng.wait_ge(s, count)

        def settle(eng, passed):
            eng.sem_inc(passed, 1)

        def run_steps(eng, step, begin=-4):
            for s in range(begin, 8):
                step(s // 8, s % 8, s)
            with eng.Fori(1, UNITS // 8 - 1) as k:
                for m in range(8):
                    step(k, m, None)
            for s in range(UNITS - 8, UNITS + 7):
                step(s // 8, s % 8, s)

        def has(s, lo, hi):
            return s is None or lo <= s < hi

        def run_expert_steps(eng, step):
            for i in range(-5, 8):
                step(i // 8, i % 8, i)
            with eng.Fori(1, EXPERT_UNITS // 8 - 2) as k:
                for m in range(8):
                    step(k, m, None)
            for i in range(EXPERT_UNITS - 16, EXPERT_UNITS + 3):
                step(i // 8, i % 8, i)

        x_tiles = x.rearrange("b (t p) d -> b p t d", p=P)
        out_tiles = out.rearrange("b (t p) d -> b p t d", p=P)
        out_rows = out.rearrange("b t d -> (b t) d")
        xn_tiles = xn_rows.rearrange("(b t p) d -> b p t d", b=NB, p=P)

        @block.sync
        def _(sp):
            for j in range(2):
                sp.sem_inc(out_out[j], 16)
            def load_x(b, slot, i):
                sp.dma_start(x_sb[:, slot, 2 * i:2 * i + 2], x_tiles[b][:, 2 * i:2 * i + 2]
                             ).then_inc(x_in[slot][i], 16)

            for n, w in enumerate((Wk, Wq, Wkp, Wqp, Wv, Wo)):
                sp.dma_start(w_nat[:, n], w.rearrange("(a p) d -> p a d", p=P)).then_inc(w_in, 16)
            for n, v in enumerate((bk, bq, bkp, bqp, bv, phase_scale, ln_g, ln_b)):
                sp.dma_start(vec_rows[2 * n:2 * n + 2, :], v.rearrange("(a p) -> a p", p=P)).then_inc(vec_in, 16)
            sp.dma_start(bo_row[:, :], bo.rearrange("(a n) -> a n", a=1)).then_inc(bo_in, 16)
            sp.dma_start(wr_nat[:, :], Wr).then_inc(wr_in, 16)
            for i in range(TPB // 2):
                load_x(0, 0, i)
            for slot in range(2):
                sp.dma_start(xn_sb[:, slot, :, D:GROW], rope.rearrange("(t p) d -> p t d", p=P)
                             ).then_inc(rope_in, 16)
            for i in range(TPB // 2):
                load_x(1, 1, i)

            def step(k, m, s):
                b = 2 * k + m // 4
                slot = (m // 4) % 2
                if s == UNITS:
                    for half in range(2):
                        sp.wait_ge(lg_out[half], 32 * NB)
                    sp.wait_ge(trig_done, 2 * UNITS)
                    for part, place in enumerate((lg, gate)):
                        sp.dma_start(place, logit_rows[part].rearrange("b e t -> (b e) t")).then_inc(lg_in, 16)
                if m % 4 == 1 and has(s, 0, UNITS):
                    sp.wait_ge(xn_done, 8 * b + 8)
                    if s is not None and s < 4:
                        sp.wait_ge(rope_in, 32)
                    sp.dma_start(xn_tiles[b], xn_sb[:, slot]).then_inc(xn_out[slot], 16)
                if m % 2 == 1 and has(s, 1, UNITS):
                    half = m // 2 % 2
                    sp.wait_ge(lg_copied, 4 * k + m // 2 + 1)
                    for part in range(2):
                        sp.dma_start(logit_rows[part, b][:, half * HALF:(half + 1) * HALF],
                                     lg_sb[part * E:(part + 1) * E, half, :]).then_inc(lg_out[half], 16)
                if has(s, 2, UNITS - 6):
                    xb = 2 * k + (m - 2) // 4
                    sp.wait_ge(base1_done, 8 * k + m - 1)
                    load_x(xb + 2, ((m - 2) // 4) % 2, (m - 2) % 4)
                if m % 2 == 0 and has(s, 8, UNITS + 7):
                    h_b, j = 2 * k + (m - 8) // 4, ((m - 8) // 2) % 2
                    sp.wait_ge(final_done, 4 * (4 * k + (m - 8) // 2) + 4)
                    sp.dma_start(out_tiles[h_b][:, TPH * j:TPH * j + TPH, :],
                                 base_sb[:, ((m - 8) // 4) % 2, TPH * j:TPH * j + TPH, :]).then_inc(out_out[j], 16)

            run_steps(sp, step)
            sp.wait_ge(base_done, UNITS)
            sp.dma_start(w_fo, Wfo.rearrange("e j d -> j e d")).then_inc(wfo_in, 16)
            for j in range(2):
                sp.wait_ge(xn_out[j], 16 * NB // 2)
            for e in range(E):
                sp.dma_start(w_qkv[:, e, :, 0:3 * HP], Wqkv[e].rearrange("(h p) j -> p h j", p=P)
                             ).then_inc(ffn_in, 16)
            for j in range(2):
                sp.wait_ge(out_out[j], 16 * NB + 16)

        @block.tensor
        def _(pe):
            pe.wait_ge(pool_set, 4)
            pe.wait_ge(w_in, 16 * 6)
            for n in range(4):
                for a in range(2):
                    for c in range(2):
                        mm = pe.transpose(ps[n][:, c * D + a * P:c * D + (a + 1) * P],
                                          w_nat[:, 2 + n, a, c * P:(c + 1) * P], ident[:, :])
                mm.then_inc(wt_mm, 1)
            pe.wait_ge(vec_in, 16 * 8)
            pe.transpose(ps[4][:, 0:16], vec_rows[:, :], ident[0:16, 0:16]).then_inc(vec_mm, 1)
            pe.wait_ge(wr_in, 16)
            for c in range(2):
                mm = pe.transpose(ps[5][:, c * E:(c + 1) * E], wr_nat[:, c * P:(c + 1) * P], ident[0:E, 0:E])
            mm.then_inc(vec_mm, 1)
            pe.wait_ge(wt_done, 4)
            pe.wait_ge(vec_done, 2)
            for n in range(2):
                for c in range(2):
                    for a in range(2):
                        mm = pe.matmul(ps[n][:, c * D:(c + 1) * D], w_nat[:, n, a, c * P:(c + 1) * P],
                                       w_tr[:, n, a, :], start=(a == 0), stop=(a == 1))
                mm.then_inc(fold_mm, 1)
            for n in range(2):
                for c in range(2):
                    for a in range(2):
                        mm = pe.matmul(ps[2][:, 2 * n + c:2 * n + c + 1], w_tr[:, n, a, c * P:(c + 1) * P],
                                       vec[:, n, a:a + 1], start=(a == 0), stop=(a == 1))
            mm.then_inc(fold_mm, 1)
            pe.wait_ge(dve_set, 6)
            for c in range(2):
                mm = pe.matmul(ps[3][:, 0:D], mean_w[:, :], wo_g[:, c, :], start=(c == 0), stop=(c == 1))
            mm.then_inc(fold_mm, 1)
            pe.wait_ge(bo_in, 16)
            for c in range(2):
                pe.matmul(ps[6][:, 0:D], lnb_cols[:, c, :], w_tr[:, 3, c, :], start=(c == 0), stop=False)
            pe.matmul(ps[6][:, 0:D], ones[0:1, :], bo_row[:, :], start=False, stop=True).then_inc(fold_mm, 1)
            pe.wait_ge(fold_done, 3)
            pe.wait_ge(split_done, 6)

            K_BANK, Q_BANK, TP_BANK, LG_BANK = ps[0], ps[1], ps[4], ps[5]

            def step(k, m, s):
                u = 8 * k + m
                b = 2 * k + m // 4
                j, f = (m // 2) % 2, m % 2
                slot = (m // 4) % 2
                if has(s, 0, UNITS):
                    wait(pe, lo_done, u - m % 2 + 2)
                    for n, bank, ready in ((0, K_BANK, k_mm), (1, Q_BANK, q_mm), (2, ps[2 + m % 2], v_mm)):
                        if n < 2:
                            wait(pe, tanh_done, 2 * u - 1 + n)
                        else:
                            wait(pe, bound_done, u - 1)
                        for g, (wp, part) in enumerate(((0, xn_lo), (1, xn_hi), (0, xn_hi))):
                            for c in range(2):
                                mm = pe.matmul(bank[:, :], w_split[:, n, c, wp, f * P:(f + 1) * P],
                                               part[:, j, c, :], start=(g + c == 0), stop=(g + c == 3))
                        mm.then_inc(ready, 1)
                    if m % 2 == 0:
                        wait(pe, lg_copied, 4 * k + m // 2)
                    for c in range(2):
                        mm = pe.matmul(LG_BANK[0:2 * E, :], wr_split[:, c, :, :].rearrange("p h e -> p (h e)"),
                                       (xn_lo, xn_hi)[m % 2][:, j, c, :], start=(m % 2 + c == 0),
                                       stop=(m % 2 + c == 2))
                    if m % 2 == 1:
                        mm.then_inc(lg_mm, 1)
                if has(s, -3, PAIRS + 1):
                    q, mq = u - 1, (m - 1) % 8
                    wait(pe, xn_done, 2 * q + 10)
                    wait(pe, hi_done, q + 4)
                    for t in range(2):
                        for c in range(2):
                            mm = pe.transpose(TP_BANK[:, c * D + t * P:c * D + (t + 1) * P],
                                              xn_sb[:, (mq // 4 + 1) % 2, 2 * (mq % 4) + t, c * P:(c + 1) * P],
                                              ident[:, :])
                    mm.then_inc(tp_mm, 1)
                first = m % 2 == 0
                if has(s, 4, UNITS + 4):
                    h, mh = 4 * k + (m - (4 if first else 5)) // 2, ((m - (4 if first else 5)) // 2) % 2
                    wait(pe, square_done, 2 * h + 2)
                    for t in range(0, 2) if first else range(2, 4):
                        bank = ps[6 + t % 2]
                        wait(pe, proj_done, 4 * h + t - 1)
                        for c in range(2):
                            pe.matmul(bank[:, 0:D + 1], retr[:, mh, c, t * P:(t + 1) * P], wo_c[:, c, :],
                                      start=(c == 0), stop=(c == 1))
                        for c in range(2):
                            mm = pe.matmul(bank[:, D + 1:D + 2], retr_sq[:, mh, c, t * P:(t + 1) * P],
                                           ones[:, 0:1], start=(c == 0), stop=(c == 1))
                        mm.then_inc(proj_mm, 1)

            run_steps(pe, step)

            pe.wait_ge(top_step, 4 * (K // 8) - 1)
            pe.wait_ge(proj_done, 4 * HALVES)
            pe.transpose(ps[0][:, 0:P], picked[:, :], ident[:, :]).then_inc(ids_mm, 1)
            pe.wait_ge(ids_done, 1)
            pe.wait_ge(wfo_in, 16)

            def expert_step(k, m, i):
                n = 8 * k + m
                if has(i, 0, EXPERT_UNITS):
                    if m == 0:
                        wait(pe, wx_lo_done, k + 2 if i is None else min(k + 2, 2 * E))
                    wait(pe, qkv_done, n)
                    if i == EXPERT_UNITS - 1:
                        wait(pe, xg_lo_done, n + 1)
                    row = k // 2 % 2 * 2
                    for g, (xpart, wp) in enumerate(((1, 0), (0, 1), (0, 0))):
                        for c in range(2):
                            mm = pe.matmul(ps[1][:, 0:QW], xg_split[:, m % 2, xpart, c * P:(c + 1) * P],
                                           w_cur[:, row + c, wp, :], start=(g + c == 0), stop=(g + c == 3))
                    mm.then_inc(qkv_mm, 1)
                if has(i, 1, EXPERT_UNITS + 1):
                    wait(pe, rope_done, n)
                    for t in range(2):
                        mm = pe.transpose(ps[2][:, t * K:(t + 1) * K], qkv[:, (m - 1) % 4, t * HP:(t + 1) * HP],
                                          ident[:, :])
                    mm.then_inc(qkt_mm, 1)
                if has(i, 2, EXPERT_UNITS + 2):
                    wait(pe, prob_done, n - 1)
                    pe.transpose(ps[4][:, 0:K], probs[:, m % 2, :], ident[:, :]).then_inc(probt_mm, 1)
                if has(i, 3, EXPERT_UNITS + 3):
                    wait(pe, av_done, n - 2)
                    if i is not None and i > EXPERT_UNITS:
                        wait(pe, xp_done, n - 4)
                    pe.matmul(ps[6 + (m - 3) % 2][:, 0:D], av_t[:, (m - 3) % 2, :],
                              w_fo[:, (k + (m - 3) // 8) // 2, :], start=True, stop=True).then_inc(xp_mm, 1)
                if has(i, -2, EXPERT_UNITS - 2):
                    g = (m + 2) % 8
                    wait(pe, xg_lo_done, n + 2)
                    pe.wait_ge(gathered[g], 16 * (k + (m + 2) // 8) + 16)
                    for c in range(2):
                        mm = pe.transpose(ps[0][:, c * P:(c + 1) * P], xg[:, g, c * P:(c + 1) * P], ident[:, :])
                    mm.then_inc(xg_mm, 1)
                if has(i, 1, EXPERT_UNITS + 1):
                    u = (m - 1) % 2
                    wait(pe, qkt_done, n)
                    pe.matmul(ps[3][:, 0:K], qk_t[:, u, 0, :], qk_t[:, u, 1, :], start=True, stop=False)
                    pe.matmul(ps[3][:, 0:K], ident_bf[:, :], causal[:, :], start=False, stop=True
                              ).then_inc(score_mm, 1)
                if has(i, 2, EXPERT_UNITS + 2):
                    wait(pe, probt_done, n - 1)
                    pe.matmul(ps[5][:, 0:K], qkv[:, (m - 2) % 4, 2 * HP:3 * HP], probs_t[:, m % 2, :],
                              start=True, stop=True).then_inc(av_mm, 1)

            run_expert_steps(pe, expert_step)

        @block.scalar
        def _(act):
            nc.scalar.preload_act_table_set("silu_and_others")
            for n in range(4):
                act.wait_ge(wt_mm, n + 1)
                nc.scalar.activation(w_tr[:, n], ps[n][:, :].rearrange("p (c d) -> p c d", c=2), ACT.Copy
                                     ).then_inc(wt_done, 1)
            act.wait_ge(vec_mm, 1)
            nc.scalar.activation(vec[:, :, :], ps[4][:, 0:16].rearrange("p (n a) -> p n a", a=2), ACT.Copy
                                 ).then_inc(vec_done, 1)
            act.wait_ge(vec_mm, 2)
            nc.scalar.activation(wr_t[:, :, :], ps[5][:, 0:2 * E].rearrange("p (c e) -> p c e", c=2), ACT.Copy
                                 ).then_inc(vec_done, 1)
            for n in range(2):
                act.wait_ge(fold_mm, n + 1)
                nc.scalar.activation(w_split[:, n, :, 0, :], ps[n][:, :].rearrange("p (c d) -> p c d", c=2),
                                     ACT.Copy).then_inc(w_hi_done, 1)

            def step(k, m, s):
                u = 8 * k + m
                b = 2 * k + m // 4
                f, slot = m % 2, (m // 4) % 2
                q, mq = u - 1, (m - 1) % 8
                if s == UNITS + 2:
                    nc.scalar.preload_act_table_set("exp_and_others")
                    act.wait_ge(gate_step, 1)
                    nc.scalar.activation(gate, lg, ACT.Exp, scale=-1.0).then_inc(exp_done, 1)
                if has(s, -3, PAIRS + 1):
                    qslot = (mq // 4 + 1) % 2
                    if mq % 4 == 0:
                        wait(act, xn_out[qslot], 16 * (k + ((m - 1) // 4 + 1) // 2))
                    wait(act, base1_done, u - 4)
                    wait(act, shift_done, q + 5)
                    for t in range(2):
                        nc.scalar.activation(xn_sb[:, qslot, 2 * (mq % 4) + t, 0:D],
                                             x_sb[:, qslot, 2 * (mq % 4) + t, :], ACT.Identity,
                                             bias=shift[:, mq % 2, t:t + 1], scale=rstd[:, mq % 2, t:t + 1]
                                             ).then_inc(xn_done, 1)
                if has(s, 0, UNITS):
                    wait(act, frac_done, u - 1)
                    for n, (bank, ready) in enumerate(((ps[0], k_mm), (ps[1], q_mm))):
                        act.wait_ge(ready, u + 1)
                        nc.scalar.activation(tanhs[:, m % 2, n, :], bank[:, :], ACT.Tanh,
                                             bias=kq_bias[:, n, f:f + 1]).then_inc(tanh_done, 1)
                if has(s, 1, UNITS + 1):
                    p = (m - 1) % 2
                    wait(act, frac_done, u)
                    wait(act, turned_done, u - 2)
                    nc.scalar.activation(frac_abs[:, p], frac[:, p], ACT.Abs).then_inc(abs_done, 1)
                    nc.scalar.activation(trig[:, p, 1], frac[:, p], ACT.Sin, scale=TWO_PI).then_inc(trig_done, 1)
                    wait(act, abs_done, u)
                    nc.scalar.activation(trig[:, p, 0], frac_abs[:, p], ACT.Sin, scale=-TWO_PI,
                                         bias=halfpi[:, 0:1]).then_inc(trig_done, 1)
                if has(s, 2, UNITS + 2):
                    wait(act, retr_done, u - 1)
                    wait(act, proj_mm, 4 * (4 * k + (m - 2) // 2) - 4)
                    r = ((m - 2) // 2) % 2
                    nc.scalar.activation(retr_sq[:, r, f, :], retr[:, r, f, :], ACT.Square
                                         ).then_inc(square_done, 1)
                first = m % 2 == 0
                if has(s, 4, UNITS + 4):
                    h, mh = 4 * k + (m - (4 if first else 5)) // 2, ((m - (4 if first else 5)) // 2) % 2
                    wait(act, final_done, 4 * h - (6 if first else 4))
                    for t in range(0, 2) if first else range(2, 4):
                        wait(act, proj_mm, 4 * h + t + 1)
                        nc.scalar.activation(proj[:, mh, t, :], ps[6 + t % 2][:, 0:D + 2], ACT.Copy
                                             ).then_inc(proj_done, 1)
                if m % 2 == 1 and has(s, 1, UNITS):
                    wait(act, lg_mm, 4 * k + m // 2 + 1)
                    wait(act, lg_out[m // 2 % 2], 32 * b)
                    nc.scalar.activation(lg_sb[:, m // 2 % 2, :], ps[5][0:2 * E, :], ACT.Copy
                                         ).then_inc(lg_copied, 1)
                if has(s, -3, PAIRS + 1):
                    wait(act, tp_mm, q + 5)
                    wait(act, lo_done, q + 3)
                    both = ps[4][:, :].rearrange("p (c d) -> p c d", c=2)
                    nc.scalar.activation(xn_stage[:, mq % 2], both, ACT.Copy).then_inc(stage_done, 1)
                    nc.scalar.activation(xn_hi[:, mq // 2 % 2, :, mq % 2 * D:(mq % 2 + 1) * D], both, ACT.Copy
                                         ).then_inc(hi_done, 1)

            run_steps(act, step)

            def expert_step(k, m, i):
                n = 8 * k + m
                if has(i, 0, EXPERT_UNITS):
                    wait(act, qkv_mm, n + 1)
                    nc.scalar.activation(qkv[:, m % 4, :], ps[1][:, 0:QW], ACT.Copy).then_inc(qkv_done, 1)
                if has(i, 2, EXPERT_UNITS + 2):
                    wait(act, probt_mm, n - 1)
                    nc.scalar.activation(probs_t[:, m % 2, :], ps[4][:, 0:K], ACT.Copy).then_inc(probt_done, 1)
                if has(i, -2, EXPERT_UNITS - 2):
                    wait(act, xg_mm, n + 3)
                    nc.scalar.activation(xg_split[:, m % 2, 0, :], ps[0][:, 0:D], ACT.Copy).then_inc(xg_hi_done, 1)
                if has(i, 1, EXPERT_UNITS + 1):
                    mp = (m - 1) % 4
                    wait(act, max_done, n)
                    nc.scalar.activation(probs[:, mp % 2, :], ps[3][:, 0:K], ACT.Exp, scale=SCALE,
                                         bias=neg_max[:, mp % 2:mp % 2 + 1], accum_out=row_sum[:, mp:mp + 1]
                                         ).then_inc(prob_done, 1)
                    wait(act, qkv_done, n)
                    nc.scalar.activation(gate_e[:, mp:mp + 1], qkv[:, mp, 3 * HP:3 * HP + 1], ACT.Exp, scale=-1.0
                                         ).then_inc(gate_done, 1)
                if has(i, 2, EXPERT_UNITS + 2):
                    wait(act, av_mm, n - 1)
                    nc.scalar.activation(av_t[:, m % 2, :], ps[5][:, 0:K], ACT.Copy).then_inc(av_done, 1)

                if m == 1 and has(i, 0, EXPERT_UNITS - 16):
                    split_hi(k + 2)

            def split_hi(r):
                nc.scalar.activation(w_cur[:, r % 4, 0, :], w_rows[:, r, :], ACT.Copy
                                     ).then_inc(wx_hi_done, 1)

            act.wait_ge(ffn_in, 16 * E)
            act.wait_ge(wr_col_done, 2)
            act.wait_ge(v_mm, UNITS)
            act.wait_ge(lg_mm, 2 * NB)
            split_hi(0)
            split_hi(1)
            act.wait_ge(ids_done, 1)
            run_expert_steps(act, expert_step)

        @block.vector
        def _(dve):
            nc.vector.memset(ones[:, :], 1.0).then_inc(dve_set, 1)
            nc.vector.memset(mean_w[:, :], 1.0 / D).then_inc(dve_set, 1)
            nc.vector.memset(halfpi[:, :], float(np.pi / 2))
            nc.vector.memset(power[:, :], -0.5)
            nc.vector.memset(restart[:, :], 1.0).then_inc(bn_done, 1)
            nc.vector.memset(wo_c[:, :, D:D + 1], 1.0)
            dve.wait_ge(bn_done, 1)
            nc.vector.memset(restart[:, :].rearrange("p (n c) -> p n c", c=CH)[:, :, 0:1], 0.0
                             ).then_inc(bn_done, 1)
            BN0 = 2

            def step(k, m, s):
                u = 8 * k + m
                f = m % 2
                has_pair, has_unit, had_unit = has(s, -4, PAIRS), has(s, 0, UNITS), has(s, 1, UNITS + 1)
                has_stats = m % 2 == 0 and has(s, 6, UNITS + 5)
                first = m % 2 == 1
                has_final = has(s, 7, UNITS + 7)
                slot = (m // 4 + 1) % 2
                p = (m - 1) % 2
                if s == UNITS + 2:
                    dve.wait_ge(lg_in, 32)
                    nc.vector.tensor_tensor(lg, lg, gate, ALU.add).then_inc(gate_step, 1)
                if s == UNITS + 3:
                    dve.wait_ge(base_done, UNITS)
                    dve.wait_ge(exp_done, 1)
                    nc.vector.tensor_scalar(gate, gate, 1.0, None, ALU.add).then_inc(gate_step, 1)
                    dve.wait_ge(gate_step, 2)
                    nc.vector.reciprocal(gate2, gate).then_inc(gate_step, 1)
                both = tanhs[:, m % 2].rearrange("p n t -> p (n t)")

                def final(t):
                    mf = m - (7 if first else 8)
                    mh = (mf // 2) % 2
                    row = base_sb[:, (mf // 4) % 2, TPH * mh + t, :]
                    nc.vector.scalar_tensor_tensor(out=row, in0=proj[:, mh, t, 0:D],
                                                   scalar=rstd2[:, mh, t:t + 1], in1=row,
                                                   op0=ALU.mult, op1=ALU.add).then_inc(final_done, 1)

                if has_pair:
                    wait(dve, x_in[slot][m % 4], 16 * (k + (m // 4 + 1) // 2) + 16)
                    for t in range(2):
                        nc.vector.bn_stats(bn[:, m % 2, t, :], x_sb[:, slot, 2 * (m % 4) + t, :]).then_inc(bn_done, 1)
                if has_unit:
                    if s == 1:
                        wait(dve, frac_done, 1)
                    wait(dve, tanh_done, 2 * u + 2)
                    nc.vector.tensor_scalar(whole[:, :], both, turns[:, f:f + 1], ROUND, ALU.mult, ALU.add
                                            ).then_inc(whole_done, 1)
                if has_pair:
                    wait(dve, shift_done, u + 3)
                    dve.wait_ge(bn_done, BN0 + 2 * u + 10)
                    settle(dve, dve_passed)
                    for t in range(2):
                        nc.vector.bn_aggr(mv[:, m % 2, t, :], bn[:, m % 2, t, :]).then_inc(mv_done, 1)
                if has_unit:
                    wait(dve, trig_done, 2 * u - 2)
                    dve.wait_ge(whole_done, u + 1)
                    nc.vector.scalar_tensor_tensor(
                        out=frac[:, m % 2].rearrange("p n t -> p (n t)"), in0=both, scalar=turns[:, f:f + 1],
                        in1=whole[:, :].bitcast(I16).rearrange("p (t w) -> p t w", w=2)[:, :, 0],
                        op0=ALU.mult, op1=ALU.subtract).then_inc(frac_done, 1)
                if has_final:
                    if first:
                        wait(dve, base_done, 8 * k + m - 5)
                        wait(dve, rstd2_done, 4 * k + (m - 7) // 2 + 1)
                    final(0 if first else 2)
                if has_stats:
                    h, mh = 4 * k + (m - 6) // 2, ((m - 6) // 2) % 2
                    total, total_sq = proj[:, mh, :, D], proj[:, mh, :, D + 1]
                    wait(dve, proj_done, 4 * h + 4)
                    nc.vector.scalar_tensor_tensor(out=m_sq[:, :], in0=total, scalar=1.0 / (D * D), in1=total,
                                                   op0=ALU.mult, op1=ALU.mult).then_inc(msq_done, 1)
                if had_unit:
                    wait(dve, v_mm, u)
                    wait(dve, trig_done, 2 * u)
                    nc.vector.scalar_tensor_tensor(
                        out=bound[:, :, :], in0=ps[2 + p][:, :].unsqueeze(1).to_broadcast([P, 2, HALF]),
                        scalar=vec[:, 4, p:p + 1], in1=trig[:, p, :, 0, :], op0=ALU.add, op1=ALU.mult
                    ).then_inc(bound_done, 1)
                if has_stats:
                    wait(dve, msq_done, h + 1)
                    nc.vector.scalar_tensor_tensor(out=var2[:, :], in0=total_sq, scalar=1.0 / D, in1=m_sq[:, :],
                                                   op0=ALU.mult, op1=ALU.subtract).then_inc(var_done, 1)
                if had_unit:
                    wait(dve, bound_done, u)
                    nc.vector.tensor_tensor_scan(memory[:, :, :].rearrange("p n t -> p (n t)"), restart[:, :],
                                                 bound[:, :, :].rearrange("p n t -> p (n t)"), 0.0,
                                                 ALU.mult, ALU.add).then_inc(memory_done, 1)
                if has_stats:
                    wait(dve, var_done, h + 1)
                    nc.vector.tensor_scalar(var2e[:, mh, :], var2[:, :], 0.0, EPS * D, ALU.max, ALU.add
                                            ).then_inc(var2e_done, 1)
                if has_final:
                    final(1 if first else 3)
                if had_unit:
                    wait(dve, retr_done, u - 2)
                    wait(dve, memory_done, u)
                    nc.vector.tensor_tensor(turned[p][:, :, :], memory[:, :, :], trig[:, p, :, 1, :], ALU.mult
                                            ).then_inc(turned_done, 1)

            for early in range(-4, 0):
                step(early // 8, early % 8, early)
            dve.wait_ge(vec_done, 1)
            dve.wait_ge(wt_done, 4)
            dve.wait_ge(dve_set, 2)
            for c in range(2):
                nc.vector.tensor_scalar(wo_g[:, c, :], w_tr[:, 3, c, :], vec[:, 6, c:c + 1], None, ALU.mult
                                        ).then_inc(dve_set, 1)
            nc.vector.tensor_scalar(turns[:, :], vec[:, 5, :], 1.0 / TWO_PI, None, ALU.mult)
            for c in range(2):
                nc.vector.tensor_scalar(lnb_cols[:, c, :], ones[:, :], vec[:, 7, c:c + 1], None, ALU.mult
                                        ).then_inc(dve_set, 1)
            def as_f32(ap):
                return ap.bitcast(F32)

            dve.wait_ge(vec_done, 2)
            nc.vector.tensor_copy(w_split[:, 2, :, 0, :], w_tr[:, 2]).then_inc(split_done, 1)
            nc.vector.tensor_copy(wr_split[:, :, 0, :], wr_t[:, :, :]).then_inc(split_done, 1)
            dve.wait_ge(split_done, 2)
            nc.vector.tensor_tensor(w_split[:, 2, :, 1, :], w_tr[:, 2], as_f32(w_split[:, 2, :, 0, :]), ALU.subtract
                                    ).then_inc(split_done, 1)
            nc.vector.tensor_tensor(wr_split[:, :, 1, :], wr_t[:, :, :], as_f32(wr_split[:, :, 0, :]), ALU.subtract
                                    ).then_inc(split_done, 1)
            for n in range(2):
                dve.wait_ge(w_hi_done, n + 1)
                nc.vector.tensor_tensor(w_split[:, n, :, 1, :], ps[n][:, :].rearrange("p (c d) -> p c d", c=2),
                                        as_f32(w_split[:, n, :, 0, :]), ALU.subtract).then_inc(split_done, 1)
            dve.wait_ge(fold_mm, 3)
            nc.vector.tensor_tensor(kq_bias[:, :, :], ps[2][:, 0:4].rearrange("p (n c) -> p n c", n=2),
                                    vec[:, 2:4, :], ALU.add).then_inc(fold_done, 1)
            dve.wait_ge(fold_mm, 4)
            nc.vector.tensor_tensor(wo_c[:, :, 0:D], wo_g[:, :, :],
                                    ps[3][:, 0:D].unsqueeze(1).to_broadcast([P, 2, D]), ALU.subtract
                                    ).then_inc(fold_done, 1)
            dve.wait_ge(fold_mm, 5)
            nc.vector.tensor_copy(const_row[:, :], ps[6][:, 0:D]).then_inc(fold_done, 1)
            dve.wait_ge(fold_done, 3)
            run_steps(dve, step, 0)

            dve.wait_ge(gate_step, 3)
            steps = 0

            def top_rounds(values, replaced_by, keep):
                nonlocal steps
                for r in range(K // 8):
                    eight = picked[:, 8 * r:8 * r + 8] if keep else top8[:, r % 2, :]
                    nc.vector.max(eight, values).then_inc(top_step, 1)
                    steps += 1
                    dve.wait_ge(top_step, steps)
                    if keep and r == K // 8 - 1:
                        break
                    nc.vector.match_replace(values, eight, values, replaced_by).then_inc(top_step, 1)
                    steps += 1
                    dve.wait_ge(top_step, steps)

            top_rounds(gate2, -1.0, False)
            dve.wait_ge(row_base_set, 2)
            nc.vector.tensor_copy(back, back_i).then_inc(gate_step, 1)
            dve.wait_ge(gate_step, 4)
            nc.vector.scalar_tensor_tensor(out=rank_key, in0=gate2, scalar=0.0, in1=back, op0=ALU.is_lt,
                                           op1=ALU.mult).then_inc(gate_step, 1)
            dve.wait_ge(gate_step, 5)
            top_rounds(rank_key, 0.0, True)
            dve.wait_ge(ids_mm, 1)
            by_expert = "p (e b) -> p e b"
            nc.vector.tensor_tensor(row_ids[:, :].rearrange(by_expert, e=E),
                                    row_base[:, :].rearrange(by_expert, e=E),
                                    ps[0][:, 0:P].rearrange("p (b e) -> p e b", e=E), ALU.subtract
                                    ).then_inc(ids_done, 1)
            for j in range(2):
                dve.wait_ge(xn_out[j], 16 * NB // 2)
            for half in range(2):
                nc.vector.tensor_copy(w_qkv[:, :, :, 3 * HP + half:3 * HP + half + 1].rearrange(
                                          "p e c o -> p e (c o)"),
                                      wr_t[:, :, :].rearrange("p c e -> p e c")).then_inc(wr_col_done, 1)

            def split_lo(r):
                wait(dve, wx_hi_done, r + 1)
                here = r % 4
                nc.vector.tensor_tensor(w_cur[:, here, 1, :], w_rows[:, r, :], w_cur[:, here, 0, :].bitcast(F32),
                                        ALU.subtract).then_inc(wx_lo_done, 1)

            dve.wait_ge(ffn_in, 16 * E)
            dve.wait_ge(wr_col_done, 2)
            split_lo(0)
            split_lo(1)
            def expert_step(k, m, i):
                n = 8 * k + m
                if has(i, 1, EXPERT_UNITS + 1):
                    wait(dve, qkt_mm, n)
                    nc.vector.tensor_copy(qk_t[:, (m - 1) % 2], ps[2][:, 0:2 * K].rearrange("p (t k) -> p t k", t=2)
                                          ).then_inc(qkt_done, 1)
                if has(i, 0, EXPERT_UNITS):
                    heads = qkv[:, m % 4, 0:2 * HP]
                    rotated = heads.rearrange("p (t h r) -> p t h r", t=2, r=RH)[:, :, 0:2, :]
                    row = xg[:, m, :]
                    cos = row[:, D:D + RH].unsqueeze(1).unsqueeze(1).to_broadcast([P, 2, 2, RH])
                    wait(dve, qkv_done, n + 1)
                    nc.vector.tensor_tensor(turn_a[:, m % 2], rotated, cos, ALU.mult).then_inc(turn_done, 1)
                    for h in range(2):
                        sin = row[:, D + (1 + h) * RH:D + (2 + h) * RH].unsqueeze(1).to_broadcast([P, 2, RH])
                        nc.vector.tensor_tensor(turn_b[:, m % 2, :, h, :], rotated[:, :, 1 - h, :], sin, ALU.mult
                                                ).then_inc(turn_done, 1)
                    dve.wait_ge(turn_done, 3 * n + 3)
                    nc.vector.tensor_tensor(
                        heads.rearrange("p (t j) -> p t j", t=2)[:, :, 0:ROT],
                        turn_a[:, m % 2].rearrange("p t h r -> p t (h r)"),
                        turn_b[:, m % 2].rearrange("p t h r -> p t (h r)"), ALU.add).then_inc(rope_done, 1)
                if has(i, 1, EXPERT_UNITS + 1):
                    u = (m - 1) % 2
                    wait(dve, score_mm, n)
                    nc.vector.tensor_scalar(scratch_s[:, :], ps[3][:, 0:K], -SCALE, None, ALU.mult, ALU.min,
                                            accum_out=neg_max[:, u:u + 1]).then_inc(max_done, 1)
                has_out = has(i, 3, EXPERT_UNITS + 3)
                if has_out:
                    u = (m - 3) % 4
                    wait(dve, gate_done, n - 2)
                    nc.vector.scalar_tensor_tensor(out=denom[:, :], in0=gate_e[:, u:u + 1], scalar=1.0,
                                                   in1=row_sum[:, u:u + 1], op0=ALU.add, op1=ALU.mult
                                                   ).then_inc(denom_done, 1)
                if has(i, -2, EXPERT_UNITS - 2):
                    wait(dve, xg_hi_done, n + 3)
                    here = xg_split[:, m % 2]
                    nc.vector.tensor_tensor(here[:, 1, :], ps[0][:, 0:D], here[:, 0, :].bitcast(F32), ALU.subtract
                                            ).then_inc(xg_lo_done, 1)
                if m == 3 and has(i, 0, EXPERT_UNITS - 16):
                    split_lo(k + 2)
                if has_out:
                    wait(dve, denom_done, n - 2)
                    nc.vector.reciprocal(row_scale[:, u % 2:u % 2 + 1], denom[:, :]).then_inc(scale_done, 1)
                    wait(dve, scattered[u], 16 * (2 * k + (m - 3) // 4))
                    wait(dve, xp_mm, n - 2)
                    wait(dve, scale_done, n - 2)
                    nc.vector.tensor_scalar(xp[:, u, :], ps[6 + u % 2][:, 0:D], row_scale[:, u % 2:u % 2 + 1], None,
                                            ALU.mult).then_inc(xp_done, 1)

            run_expert_steps(dve, expert_step)

        @block.gpsimd
        def _(pool):
            nc.gpsimd.memset(ident[:, :], 0.0).then_inc(pool_set, 1)
            nc.gpsimd.memset(causal[:, :], 0.0).then_inc(pool_set, 1)
            pool.wait_ge(pool_set, 2)
            nc.gpsimd.affine_select(out=ident[:, :], in_=ident[:, :], compare_op=ALU.not_equal, fill=1.0, base=0,
                                    pattern=[[-1, P]], channel_multiplier=1).then_inc(pool_set, 1)
            nc.gpsimd.affine_select(out=causal[:, :], in_=causal[:, :], compare_op=ALU.is_ge, fill=MASKED, base=0,
                                    pattern=[[-1, K]], channel_multiplier=1).then_inc(pool_set, 1)
            pool.wait_ge(pool_set, 4)
            nc.gpsimd.tensor_copy(ident_bf[:, :], ident[:, :]).then_inc(pool_set, 1)
            nc.gpsimd.iota(row_base[:, :], pattern=[[0, E], [SEQ, NB]], base=SEQ, channel_multiplier=0
                           ).then_inc(row_base_set, 1)
            pool.wait_ge(bn_done, 2)

            def step(k, m, s):
                u = 8 * k + m
                if has(s, -2, PAIRS + 2):
                    mq = (m - 2) % 8
                    wait(pool, hi_done, u + 3)
                    place = (slice(None), mq // 2 % 2, slice(None), slice(mq % 2 * D, (mq % 2 + 1) * D))
                    nc.gpsimd.tensor_tensor(xn_lo[place], xn_stage[:, mq % 2], xn_hi[place].bitcast(F32),
                                            ALU.subtract).then_inc(lo_done, 1)
                if has(s, -4, PAIRS):
                    wait(pool, mv_done, 2 * u + 10)
                    wait(pool, xn_done, 2 * u + 6)
                    settle(pool, pool_passed)
                    nc.gpsimd.tensor_scalar(ve[:, m % 2, :], mv[:, m % 2, :, 1], EPS, None, ALU.add
                                            ).then_inc(ve_done, 1)
                    nc.gpsimd.tensor_scalar(neg_mean[:, m % 2, :], mv[:, m % 2, :, 0], -1.0, None, ALU.mult
                                            ).then_inc(ve_done, 1)
                    pool.wait_ge(ve_done, 2 * u + 10)
                    nc.gpsimd.tensor_tensor(rstd[:, m % 2, :], ve[:, m % 2, :], power[:, 0:2], ALU.pow
                                            ).then_inc(rstd_done, 1)
                    pool.wait_ge(rstd_done, u + 5)
                    nc.gpsimd.tensor_tensor(shift[:, m % 2, :], neg_mean[:, m % 2, :], rstd[:, m % 2, :], ALU.mult
                                            ).then_inc(shift_done, 1)
                if has(s, 2, UNITS + 2):
                    b, slot, i = 2 * k + (m - 2) // 4, ((m - 2) // 4) % 2, (m - 2) % 4
                    if i == 0:
                        wait(pool, xn_done, 8 * b + 8)
                    if i % 2 == 0:
                        wait(pool, out_out[i // 2], 16 * b)
                    tiles = base_sb[:, slot, 2 * i:2 * i + 2]
                    nc.gpsimd.tensor_tensor(tiles, x_sb[:, slot, 2 * i:2 * i + 2],
                                            xn_sb[:, slot, 2 * i:2 * i + 2, 0:D], ALU.add).then_inc(base1_done, 1)
                    wait(pool, base1_done, u - 1)
                    if s == 2:
                        pool.wait_ge(fold_done, 3)
                    nc.gpsimd.tensor_tensor(tiles, tiles, const_row[:, :].unsqueeze(1).to_broadcast([P, 2, D]),
                                            ALU.add).then_inc(base_done, 1)
                if has(s, 1, UNITS + 1):
                    wait(pool, turned_done, u)
                    wait(pool, proj_mm, 4 * (4 * k + (m - 1) // 2) - 4)
                    nc.gpsimd.tensor_tensor(retr[:, (m - 1) // 2 % 2, (m - 1) % 2, :], turned[(m - 1) % 2][:, 0, :],
                                            turned[(m - 1) % 2][:, 1, :], ALU.add).then_inc(retr_done, 1)
                if m % 2 == 0 and has(s, 6, UNITS + 5):
                    h, mh = 4 * k + (m - 6) // 2, ((m - 6) // 2) % 2
                    wait(pool, var2e_done, h + 1)
                    nc.gpsimd.tensor_tensor(rstd2[:, mh, :], var2e[:, mh, :], power[:, 0:TPH], ALU.pow
                                            ).then_inc(rstd2_done, 1)

            run_steps(pool, step)
            for j in range(2):
                pool.wait_ge(out_out[j], 16 * NB + 16)
                pool.wait_ge(xn_out[j], 16 * NB // 2)
            nc.gpsimd.iota(back_i, pattern=[[-1, SEQ]], base=SEQ, channel_multiplier=0).then_inc(row_base_set, 1)
            pool.wait_ge(ids_done, 1)

            def expert_step(k, m, i):
                n = 8 * k + m
                if has(i, -5, EXPERT_UNITS - 5):
                    g = (m + 5) % 8
                    if m % 4 == 0 or i == -5:
                        count = 4 - m % 4 if i is None else min(4 - m % 4, EXPERT_UNITS - 5 - i)
                        wait(pool, xg_mm, n + 1)
                        nc.gpsimd.tensor_copy(ids_in[:, m:m + count], row_ids[:, bass.ds(n + 5, count)]
                                              ).then_inc(ids_in_set, 1)
                        pool.wait_ge(ids_in_set, 2 * k + m // 4 + 3)
                    wait(pool, rope_done, n - 2)
                    settle(pool, pool_passed)
                    nc.gpsimd.indirect_dma_start(
                        out=xg[:, g, :], out_offset=None, in_=xn_rows,
                        in_offset=bass.IndirectOffsetOnAxis(ap=ids_in[:, m:m + 1].bitcast(U32), axis=0)
                    ).then_inc(gathered[g], 16)
                if has(i, 3, EXPERT_UNITS + 3):
                    g = (m - 3) % 4
                    ks = 2 * k + (m - 3) // 4
                    wait(pool, scattered[g], 16 * ks)
                    if m % 4 == 0 or i == 3:
                        count = 4 - m % 4 if i is None else min(4 - m % 4, EXPERT_UNITS + 3 - i)
                        nc.gpsimd.tensor_copy(ids_out[:, m:m + count], row_ids[:, bass.ds(n - 3, count)]
                                              ).then_inc(ids_out_set, 1)
                        pool.wait_ge(ids_out_set, 2 * k + m // 4 + 1)
                    wait(pool, xp_done, n - 2)
                    settle(pool, pool_passed)
                    nc.gpsimd.indirect_dma_start(
                        out=out_rows, out_offset=bass.IndirectOffsetOnAxis(ap=ids_out[:, m:m + 1].bitcast(U32),
                                                                           axis=0),
                        in_=xp[:, g, :], in_offset=None, compute_op=ALU.add).then_inc(scattered[g], 16)

            run_expert_steps(pool, expert_step)
            for g in range(4):
                pool.wait_ge(scattered[g], 16 * EXPERT_UNITS // 4)


def rope_rows():
    inv_freq = (1.0 / np.float32(10000.0) ** (np.arange(RH, dtype=np.float32) * np.float32(2.0) / np.float32(ROT))
                ).astype(np.float32)
    angle = np.arange(SEQ, dtype=np.float32)[:, None] * inv_freq
    cos, sin = np.cos(angle), np.sin(angle)
    return np.ascontiguousarray(np.concatenate([cos, -sin, sin], axis=1).astype(np.float32))


_INS = ["L0_attn_x", "L0_attn_Wk", "L0_attn_bk", "L0_attn_Wv", "L0_attn_bv", "L0_attn_Wq", "L0_attn_bq",
        "L0_attn_Wkp", "L0_attn_bkp", "L0_attn_Wqp", "L0_attn_bqp", "L0_attn_phase_scale", "L0_attn_ln_g",
        "L0_attn_ln_b", "L0_attn_Wo", "L0_attn_bo", "L0_ffn_Wr", "L0_ffn_Wqkv", "L0_ffn_Wo"]


def kernel(**inputs):
    import concourse.bacc as bacc
    from concourse.bass_utils import run_bass_kernel_spmd

    nc = bacc.Bacc("TRN2", target_bir_lowering=False, num_devices=1)
    arrays, args = {}, []
    for name in _INS:
        a = np.ascontiguousarray(inputs[name])
        arrays[f"in_{name}"] = a
        args.append(nc.dram_tensor(f"in_{name}", a.shape, mybir.dt.from_np(a.dtype), kind="ExternalInput").ap())
    arrays["rope_rows"] = rope_rows()
    args.append(nc.dram_tensor("rope_rows", [SEQ, 3 * RH], F32, kind="ExternalInput").ap())
    args.append(nc.dram_tensor("out_x", [NB, SEQ, D], F32, kind="ExternalOutput").ap())
    build(nc, *args)
    r = run_bass_kernel_spmd(nc, [arrays], core_ids=[0])
    return r.results[0]["out_x"]
```
